# Optimizing a Trainium2 kernel written in Bass

```python
import numpy as np
import jax
import jax.numpy as jnp

def _softmax(x, axis=-1):
    return jax.nn.softmax(x, axis=axis)

def _gelu(x):
    return jax.nn.gelu(x, approximate=True)

def _silu(x):
    return jax.nn.silu(x)

def _sigmoid(x):
    return jax.nn.sigmoid(x)

def _layernorm(x, axis=-1, eps=1e-05):
    m = jnp.mean(x, axis=axis, keepdims=True)
    v = jnp.var(x, axis=axis, keepdims=True)
    return (x - m) / jnp.sqrt(v + eps)

def _scatter_add(tgt, idx, src, axis=0):
    return tgt.at[idx].add(src)

def _segment_sum(src, seg, n):
    return jax.ops.segment_sum(src, seg, n)
kernel_name = 'mk_adj_preln_d2_adj_r2_e12f38'

def setup_inputs(seed: int=0):
    np.random.seed(seed)
    _w = jnp.asarray

    def _rec_inputs():
        import jax
        import jax.numpy as jnp
        _gk = jax.random.key(seed)
        x = -8.776e-05 + 1 * jax.random.normal(jax.random.fold_in(_gk, 1), (10000, 128), jnp.float32)
        _w = (1.0 + jnp.arange(10000, dtype=jnp.float32)) ** (-0.5)
        _w = _w / _w.mean()
        _pij = jnp.clip(0.0004 * _w[:, None] * _w[None, :], 0.0, 1.0)
        _a = jax.random.uniform(jax.random.fold_in(_gk, 2), (10000, 10000)) < _pij
        _a = jnp.logical_or(_a, jnp.eye(10000, dtype=bool))
        _af = _a.astype(jnp.float32)
        _af = _af * jax.random.uniform(jax.random.fold_in(_gk, 3), (10000, 10000), jnp.float32, 0.05, 1)
        adj = _af
        return (x, adj)
    x, adj = _rec_inputs()

    def _L0_gnn_setup():
        import jax, jax.numpy as jnp
        import numpy as np
        N_USER = 10000
        N_ITEM = 10000
        HID = 128
        key = jax.random.key(seed)
        k1, k2, k3, k4, k5, k6, k7 = jax.random.split(key, 7)
        scale = 1.0 / np.sqrt(HID)
        return {'user_feat': jax.random.normal(k1, (N_USER, HID), dtype=jnp.float32), 'item_feat': jax.random.normal(k2, (N_ITEM, HID), dtype=jnp.float32), 'adj': jax.random.uniform(k3, (N_USER, N_ITEM), dtype=jnp.float32), 'W_item': jax.random.uniform(k4, (HID, HID), dtype=jnp.float32, minval=-scale, maxval=scale), 'b_item': jax.random.uniform(k5, (HID,), dtype=jnp.float32, minval=-scale, maxval=scale), 'W_user': jax.random.uniform(k6, (HID, HID), dtype=jnp.float32, minval=-scale, maxval=scale), 'b_user': jax.random.uniform(k7, (HID,), dtype=jnp.float32, minval=-scale, maxval=scale)}
    _L0_gnn_all = _L0_gnn_setup()
    _L0_gnn_in = {k: v for k, v in _L0_gnn_all.items() if k in ('item_feat', 'W_item', 'b_item', 'W_user', 'b_user')}
    del _L0_gnn_all

    def _L1_gnn_setup():
        import jax, jax.numpy as jnp
        import numpy as np
        from jax import lax
        D_MODEL = 128
        D_STATE = 16
        D_CONV = 4
        EXPAND = 2
        D_INNER = EXPAND * D_MODEL
        DT_RANK = (D_MODEL + 15) // 16
        N = 2048
        EPS = 1e-05

        def _mamba(h, w_in, conv_w, conv_b, w_xp, w_dt, b_dt, A_log, D_skip, w_out):
            L = h.shape[0]
            xz = h @ w_in
            xc, z = (xz[:, :D_INNER], xz[:, D_INNER:])
            xpad = jnp.pad(xc, ((D_CONV - 1, 0), (0, 0)))
            xconv = sum((xpad[k:k + L] * conv_w[:, k] for k in range(D_CONV))) + conv_b
            u = jax.nn.silu(xconv)
            dbc = u @ w_xp
            dt = jax.nn.softplus(dbc[:, :DT_RANK] @ w_dt + b_dt)
            B = dbc[:, DT_RANK:DT_RANK + D_STATE]
            C = dbc[:, DT_RANK + D_STATE:]
            A = -jnp.exp(A_log)
            dA = jnp.exp(dt[:, :, None] * A[None])
            dBu = dt[:, :, None] * B[:, None, :] * u[:, :, None]

            def step(hst, inp):
                dAt, dBut, Ct = inp
                hst = dAt * hst + dBut
                return (hst, hst @ Ct)
            _, ys = lax.scan(step, jnp.zeros((D_INNER, D_STATE), h.dtype), (dA, dBu, C))
            y = ys + u * D_skip
            y = y * jax.nn.silu(z)
            return y @ w_out
        key = jax.random.key(seed)
        ks = jax.random.split(key, 16)
        x = jax.random.normal(ks[0], (N, D_MODEL), dtype=jnp.float32)
        a = jax.random.uniform(ks[1], (N, N), dtype=jnp.float32)
        adj = a / a.sum(axis=1, keepdims=True)
        s = lambda fi, fo: 1.0 / np.sqrt(fi)
        gcn_w = jax.random.uniform(ks[2], (D_MODEL, D_MODEL), jnp.float32, -s(D_MODEL, 0), s(D_MODEL, 0))
        gcn_b = jnp.zeros((D_MODEL,), jnp.float32)
        ln_g = jnp.ones((D_MODEL,), jnp.float32)
        ln_b = jnp.zeros((D_MODEL,), jnp.float32)
        w_in = jax.random.normal(ks[3], (D_MODEL, 2 * D_INNER), jnp.float32) * s(D_MODEL, 0)
        conv_w = jax.random.normal(ks[4], (D_INNER, D_CONV), jnp.float32) * s(D_CONV, 0)
        conv_b = jnp.zeros((D_INNER,), jnp.float32)
        w_xp = jax.random.normal(ks[5], (D_INNER, DT_RANK + 2 * D_STATE), jnp.float32) * s(D_INNER, 0)
        w_dt = jax.random.normal(ks[6], (DT_RANK, D_INNER), jnp.float32) * s(DT_RANK, 0)
        b_dt = jnp.log(jnp.expm1(jnp.exp(jax.random.uniform(ks[7], (D_INNER,), jnp.float32, np.log(0.001), np.log(0.1)))))
        A_log = jnp.log(jnp.broadcast_to(jnp.arange(1, D_STATE + 1, dtype=jnp.float32), (D_INNER, D_STATE)))
        D_skip = jnp.ones((D_INNER,), jnp.float32)
        w_out = jax.random.normal(ks[8], (D_INNER, D_MODEL), jnp.float32) * s(D_INNER, 0)
        return dict(x=x, adj=adj, gcn_w=gcn_w, gcn_b=gcn_b, ln_g=ln_g, ln_b=ln_b, w_in=w_in, conv_w=conv_w, conv_b=conv_b, w_xp=w_xp, w_dt=w_dt, b_dt=b_dt, A_log=A_log, D_skip=D_skip, w_out=w_out)
    _L1_gnn_all = _L1_gnn_setup()
    _L1_gnn_in = {k: v for k, v in _L1_gnn_all.items() if k in ('gcn_w', 'gcn_b', 'ln_g', 'ln_b', 'w_in', 'conv_w', 'conv_b', 'w_xp', 'w_dt', 'b_dt', 'A_log', 'D_skip', 'w_out')}
    del _L1_gnn_all
    return {'x': x, 'adj': adj, 'L0_gnn_item_feat': _L0_gnn_in['item_feat'], 'L0_gnn_W_item': _L0_gnn_in['W_item'], 'L0_gnn_b_item': _L0_gnn_in['b_item'], 'L0_gnn_W_user': _L0_gnn_in['W_user'], 'L0_gnn_b_user': _L0_gnn_in['b_user'], 'L1_gnn_gcn_w': _L1_gnn_in['gcn_w'], 'L1_gnn_gcn_b': _L1_gnn_in['gcn_b'], 'L1_gnn_ln_g': _L1_gnn_in['ln_g'], 'L1_gnn_ln_b': _L1_gnn_in['ln_b'], 'L1_gnn_w_in': _L1_gnn_in['w_in'], 'L1_gnn_conv_w': _L1_gnn_in['conv_w'], 'L1_gnn_conv_b': _L1_gnn_in['conv_b'], 'L1_gnn_w_xp': _L1_gnn_in['w_xp'], 'L1_gnn_w_dt': _L1_gnn_in['w_dt'], 'L1_gnn_b_dt': _L1_gnn_in['b_dt'], 'L1_gnn_A_log': _L1_gnn_in['A_log'], 'L1_gnn_D_skip': _L1_gnn_in['D_skip'], 'L1_gnn_w_out': _L1_gnn_in['w_out']}

def reference(x, adj, L0_gnn_item_feat, L0_gnn_W_item, L0_gnn_b_item, L0_gnn_W_user, L0_gnn_b_user, L1_gnn_gcn_w, L1_gnn_gcn_b, L1_gnn_ln_g, L1_gnn_ln_b, L1_gnn_w_in, L1_gnn_conv_w, L1_gnn_conv_b, L1_gnn_w_xp, L1_gnn_w_dt, L1_gnn_b_dt, L1_gnn_A_log, L1_gnn_D_skip, L1_gnn_w_out):
    import jax
    import jax.numpy as jnp

    def _L0_gnn_ref(user_feat, item_feat, adj, W_item, b_item, W_user, b_user):
        import jax, jax.numpy as jnp
        import numpy as np
        N_USER = 10000
        N_ITEM = 10000
        HID = 128
        h = item_feat @ W_item.T + b_item
        b = user_feat @ W_user.T + b_user
        return jax.nn.relu(adj @ h + b)

    def _L1_gnn_ref(x, adj, gcn_w, gcn_b, ln_g, ln_b, w_in, conv_w, conv_b, w_xp, w_dt, b_dt, A_log, D_skip, w_out):
        import jax, jax.numpy as jnp
        import numpy as np
        from jax import lax
        D_MODEL = 128
        D_STATE = 16
        D_CONV = 4
        EXPAND = 2
        D_INNER = EXPAND * D_MODEL
        DT_RANK = (D_MODEL + 15) // 16
        N = 2048
        EPS = 1e-05

        def _mamba(h, w_in, conv_w, conv_b, w_xp, w_dt, b_dt, A_log, D_skip, w_out):
            L = h.shape[0]
            xz = h @ w_in
            xc, z = (xz[:, :D_INNER], xz[:, D_INNER:])
            xpad = jnp.pad(xc, ((D_CONV - 1, 0), (0, 0)))
            xconv = sum((xpad[k:k + L] * conv_w[:, k] for k in range(D_CONV))) + conv_b
            u = jax.nn.silu(xconv)
            dbc = u @ w_xp
            dt = jax.nn.softplus(dbc[:, :DT_RANK] @ w_dt + b_dt)
            B = dbc[:, DT_RANK:DT_RANK + D_STATE]
            C = dbc[:, DT_RANK + D_STATE:]
            A = -jnp.exp(A_log)
            dA = jnp.exp(dt[:, :, None] * A[None])
            dBu = dt[:, :, None] * B[:, None, :] * u[:, :, None]

            def step(hst, inp):
                dAt, dBut, Ct = inp
                hst = dAt * hst + dBut
                return (hst, hst @ Ct)
            _, ys = lax.scan(step, jnp.zeros((D_INNER, D_STATE), h.dtype), (dA, dBu, C))
            y = ys + u * D_skip
            y = y * jax.nn.silu(z)
            return y @ w_out
        h = jax.nn.relu(adj @ x @ gcn_w + gcn_b)
        mu = h.mean(-1, keepdims=True)
        var = h.var(-1, keepdims=True)
        h = (h - mu) * lax.rsqrt(var + EPS) * ln_g + ln_b
        return _mamba(h, w_in, conv_w, conv_b, w_xp, w_dt, b_dt, A_log, D_skip, w_out)
    h = jnp.maximum(_layernorm(x, axis=-1), 0.0)
    x = x + _L0_gnn_ref(h, L0_gnn_item_feat, adj, L0_gnn_W_item, L0_gnn_b_item, L0_gnn_W_user, L0_gnn_b_user)
    h = jnp.maximum(_layernorm(x, axis=-1), 0.0)
    x = x + _L1_gnn_ref(h, adj, L1_gnn_gcn_w, L1_gnn_gcn_b, L1_gnn_ln_g, L1_gnn_ln_b, L1_gnn_w_in, L1_gnn_conv_w, L1_gnn_conv_b, L1_gnn_w_xp, L1_gnn_w_dt, L1_gnn_b_dt, L1_gnn_A_log, L1_gnn_D_skip, L1_gnn_w_out)
    return x

_drawn_inputs = setup_inputs


def setup_inputs(seed=0):
    import zlib

    import numpy as np

    out = dict(_drawn_inputs(seed))
    spreads = {'L1_gnn_gcn_b': (0.0, 0.1),
     'L1_gnn_ln_g': (1.0, 0.2),
     'L1_gnn_ln_b': (0.0, 0.1),
     'L1_gnn_conv_b': (0.0, 0.1),
     'L1_gnn_D_skip': (1.0, 0.2)}
    factors = {}
    for name, (base, spread) in spreads.items():
        noise = np.random.default_rng([zlib.crc32(name.encode()), seed]).standard_normal(out[name].shape)
        drawn = base * np.exp(spread * noise) if base else spread * noise
        out[name] = jnp.asarray(drawn.astype(out[name].dtype))
    for name, factor in factors.items():
        out[name] = (out[name] * factor).astype(out[name].dtype)
    return out
```

```python
from contextlib import ExitStack

import concourse.bass as bass
from concourse import mybir

ALU = mybir.AluOpType
ACT = mybir.ActivationFunctionType
F32 = mybir.dt.float32
BF16 = mybir.dt.bfloat16

CONSTS = 11
P = 128
D = 128
NODES = 10000
CW = 512
NC = -(-NODES // CW)
LASTW = NODES - (NC - 1) * CW
FULL = NODES // P
REST = NODES - FULL * P
GT = 6
NG = FULL // GT
RING = 3
STEPS = 16
NS = 16
DI = 256
HALF = DI // P
RANK = 8
TAPS = 4
EPS = 1e-5

FRONT_ACT = ["h", "square", "lnvar", "rstd", "norm", "xc0", "xc1", "tap0", "tap1", "z0", "z1",
             "xabs", "xexp", "xln", "xsig", "dtrow", "bc_hi", "bc_mid",
             "raw0", "abs0", "raw1", "abs1", "dexp", "dln", "zabs", "zexp", "zln", "zsig"]
FRONT_DVE = ["centre", "scaled", "conv0", "conv1", "conv2", "conv3", "conv4", "conv5", "xmin",
             "bc_rest", "bc_low", "one_e", "dt", "zmin"]
FRONT_POOL = ["u", "lost", "log", "dtu", "gate"]
FRONT_PE = ["gcn", "mean", "var", "xc0", "xc1", "z0", "z1", "dbc", "dt0", "dt1"]


class Count:

    def __init__(self, i, a, b):
        self.i, self.a, self.b = i, a, b

    def __add__(self, n):
        return Count(self.i, self.a, self.b + n)

    def __sub__(self, n):
        return Count(self.i, self.a, self.b - n)

    def __mul__(self, n):
        return Count(self.i, self.a * n, self.b * n)


def val(c):
    if isinstance(c, Count):
        assert c.b > 0, "a wait that isn't above zero in the first turn"
        return c.i * c.a + c.b if c.b else c.i * c.a
    return c


def act_at(c, name):
    return c * len(FRONT_ACT) + FRONT_ACT.index(name) + 1


def dve_at(c, name):
    return c * len(FRONT_DVE) + FRONT_DVE.index(name) + 1


def pool_at(c, name):
    return c * len(FRONT_POOL) + FRONT_POOL.index(name) + 1


def pe_at(c, name):
    return c * len(FRONT_PE) + FRONT_PE.index(name) + 1


def known(c, least):
    return c is not None and (not isinstance(c, int) or c >= least)


def row_tiles(w):
    return [(r, min(P, w - r * P)) for r in range(-(-w // P))]


def row_parts(w):
    whole, rest = divmod(w, P)
    return [(P, 0, whole)] + ([(rest, whole, whole + 1)] if rest else [])


def gnn_mamba(nc, adj_main, adj_last, adj_rest, x, featT, w_itemT, b_item, w_userT, b_user,
              gcn_w, gcn_b, ln_g, ln_b, w_in, conv_w, conv_b, w_xp, w_dt, b_dt, A_log, D_skip, w_out, out):
    with ExitStack() as ctx:
        def sb(name, shape, dt=F32):
            return ctx.enter_context(nc.sbuf_tensor(name, shape, dt))

        def sem(name):
            return ctx.enter_context(nc.semaphore(name))

        x1_dram = nc.dram_tensor("x1_dram", (NODES, D), F32, kind="Internal").ap()

        adjb = sb("adjb", [P, RING + 1, GT, CW])
        adjr = sb("adjr", [REST, 2, CW])
        item_h = sb("item_h", [P, (FULL + 1) * D])
        node_h = sb("node_h", [P, (FULL + 1) * D])
        spare = sb("spare", [P, 14880])
        pick = sb("pick", [P, 2 * NS, P], BF16)
        ident = sb("ident", [P, P])
        mean_w = sb("mean_w", [P, P])
        gcn_w_s = sb("gcn_w_s", [P, D])
        w_in_s = sb("w_in_s", [P, 2 * DI])
        w_xp_s = sb("w_xp_s", [P, HALF, P])
        w_dt_s = sb("w_dt_s", [RANK, DI])
        w_out_s = sb("w_out_s", [P, HALF, D])
        bias_rows = sb("bias_rows", [1, 2, D])
        ones = sb("ones", [1, P])
        eps_c = sb("eps_c", [P, 1])
        gcn_b_c = sb("gcn_b_c", [P, 1])
        ln_g_c = sb("ln_g_c", [P, 1])
        ln_b_c = sb("ln_b_c", [P, 1])
        conv_w_c = sb("conv_w_c", [P, HALF, TAPS])
        conv_b_c = sb("conv_b_c", [P, HALF])
        b_dt_c = sb("b_dt_c", [P, HALF])
        skip_c = sb("skip_c", [P, HALF])
        A_c = sb("A_c", [P, HALF, NS])
        Aneg_c = sb("Aneg_c", [P, HALF, NS])
        state = sb("state", [P, NS, HALF])
        stats = sb("stats", [P, 2, 4, 6])
        moments = sb("moments", [P, 2, 4, 2])
        lnv = sb("lnv", [P, 2, 4])
        rstd4 = sb("rstd4", [P, 2, 4])
        nmr4 = sb("nmr4", [P, 2, 4])

        room = {"item_h": [item_h, 0], "spare": [spare, 0]}

        def take(where, n):
            t, at = room[where]
            room[where][1] = at + n
            return t[:, at:at + n]

        def pair(where):
            return take(where, HALF * CW).rearrange("p (h w) -> p h w", h=HALF)

        u = [pair("item_h") for _ in range(2)]
        dt = [pair("item_h") for _ in range(2)]
        dtu = [pair("item_h") for _ in range(2)]
        gate = [pair("item_h") for _ in range(2)]
        tb = pair("item_h")
        decay = [pair("spare") for _ in range(2)]
        drive = [pair("spare") for _ in range(4)]
        hist = [pair("spare") for _ in range(2)]
        ysum = [pair("spare") for _ in range(2)]
        ta = pair("spare")
        gh = pair("spare")
        g_s, h_s = gh[:, 0, :], gh[:, 1, :]
        parts = [t.bitcast(BF16) for t in (take("spare", CW // 2), take("spare", CW // 2))]
        rest_s = take("spare", CW)
        dtrow = rest_s[0:RANK, :]
        x1_in = take("spare", CW).rearrange("p (r d) -> p r d", d=D)
        xc = take("spare", HALF * (CW + TAPS - 1)).rearrange("p (h w) -> p h w", h=HALF)
        quad = lambda t, k: t[:, k, :].rearrange("p (r d) -> p r d", d=D)
        x_in = [quad(hist[0], k) for k in range(2)]
        user_h = quad(hist[1], 0)
        aggT = hist[1][:, 1, :]
        w_itemT_s, w_userT_s = decay[0][:, 0, 0:D], decay[0][:, 0, D:2 * D]
        bias_b = decay[0][:, 1, 0:2 * D].rearrange("p (a d) -> p a d", a=2)
        userT = [ysum[0][:, k, :] for k in range(2)]
        x1_s = [quad(ysum[1], k) for k in range(2)]

        def bank(name):
            return ctx.enter_context(nc.psum_tensor(name, [P, CW], F32))

        acc = [bank(f"acc{i}") for i in range(2)]
        misc = [bank(f"misc{i}") for i in range(2)]
        b_all = [bank(f"b_all{i}") for i in range(2)]
        c_all = [bank(f"c_all{i}") for i in range(2)]

        feat_in = sem("feat_in")
        weights_in = sem("weights_in")
        weights1_in = sem("weights1_in")
        consts = sem("consts")
        bias_spread = sem("bias_spread")
        bias_kept = sem("bias_kept")
        item_done = sem("item_done")
        item_kept = sem("item_kept")
        slot_in = [sem(f"adj_in{i}") for i in range(RING + 1)]
        rest_in = sem("rest_in")
        group_used = sem("group_used")
        acc_full = sem("acc_full")
        acc_read = sem("acc_read")
        x_loaded = sem("x_loaded")
        user_bn = sem("user_bn")
        x1_bn = sem("x1_bn")
        user_stat = sem("user_stat")
        user_lnv = sem("user_lnv")
        user_rstd = sem("user_rstd")
        user_shift = sem("user_shift")
        user_ready = sem("user_ready")
        userT_done = sem("userT_done")
        userT_kept = sem("userT_kept")
        rows_done = sem("rows_done")
        rows_biased = sem("rows_biased")
        x1_ready = sem("x1_ready")
        x1_stat = sem("x1_stat")
        x1_lnv = sem("x1_lnv")
        x1_rstd = sem("x1_rstd")
        x1_shift = sem("x1_shift")
        node_ready = sem("node_ready")
        x1_stored = sem("x1_stored")
        a_exp = sem("a_exp")
        a_neg = sem("a_neg")
        front_act = sem("front_act")
        front_dve = sem("front_dve")
        front_pool = sem("front_pool")
        front_pe = sem("front_pe")
        conv_tail = sem("conv_tail")
        b_spread = sem("b_spread")
        c_spread = sem("c_spread")
        decay_ready = sem("decay_ready")
        drive_ready = sem("drive_ready")
        scanned = sem("scanned")
        state_kept = sem("state_kept")
        weighed = sem("weighed")
        summed = sem("summed")
        skip_added = sem("skip_added")
        gated = sem("gated")
        projected = sem("projected")
        out_ready = sem("out_ready")
        x1_back = sem("x1_back")
        out_stored = sem("out_stored")

        block = ctx.enter_context(nc.Block())

        def width(c):
            return LASTW if isinstance(c, int) and c == NC - 1 else CW

        def rounds(fori, one_round):
            def at(f):
                one_round(*[k if 0 <= k < NC else None for k in (f + 1, f, f - 1, f - 2)], f % 2)

            for f in range(-1, 4):
                at(f)
            with fori(0, (NC - 6) // 2) as i:
                for k in range(2):
                    one_round(Count(i, 2, 5 + k), Count(i, 2, 4 + k), Count(i, 2, 3 + k), Count(i, 2, 2 + k), k)
            for f in range(NC - 2, NC + 2):
                at(f)

        def chunks0(fori, one_chunk):
            for c in range(3):
                one_chunk(c, c % 2)
            with fori(0, (NC - 4) // 2) as i:
                one_chunk(Count(i, 2, 3), 1)
                one_chunk(Count(i, 2, 4), 0)
            one_chunk(NC - 1, (NC - 1) % 2)

        def scan_index(s, f, n):
            return (s, n) if n < NS else (f, n - NS)

        def settled(engine):
            engine.wait_ge(consts, CONSTS)

        @block.sync
        def _(sp):
            sp.dma_start(w_itemT_s[:, :], w_itemT).then_inc(weights_in, 16)
            sp.dma_start(bias_rows[:, 0, :], b_item.rearrange("(a n) -> a n", a=1)).then_inc(weights_in, 16)
            sp.dma_start(bias_rows[:, 1, :], b_user.rearrange("(a n) -> a n", a=1)).then_inc(weights_in, 16)
            sp.dma_start(w_userT_s[:, :], w_userT).then_inc(weights_in, 16)
            cut = 4 * D * 5
            for k in range(4):
                e = min((k + 1) * cut, NODES)
                sp.dma_start(node_h[:, k * cut:e], featT[:, k * cut:e]).then_inc(feat_in, 16)
                sp.wait_ge(feat_in, val((k + 1) * 16))

            def load_x(c, par):
                settled(sp)
                if known(c, 2):
                    sp.wait_ge(x1_ready, val(c - 1))
                if known(c, 1):
                    sp.wait_ge(x_loaded, val(c * 16))
                w = width(c)
                if w == CW:
                    sp.dma_start(x_in[par], x[bass.ds(val(c * CW), CW), :].rearrange("(r p) d -> p r d", p=P)
                                 ).then_inc(x_loaded, 16)
                else:
                    whole = w // P * P
                    sp.dma_start(x_in[par][:, 0:w // P, :], x[c * CW:c * CW + whole, :].rearrange(
                        "(r p) d -> p r d", p=P)).then_inc(x_loaded, 16)
                    sp.dma_start(x_in[par][0:w - whole, w // P, :], x[c * CW + whole:NODES, :]
                                 ).then_inc(x_loaded, 16)

            def load_adj(layer, c, g, par):
                cc = c + layer * NC
                slot = g % RING if g < NG - 1 else RING
                if g == NG - 1:
                    if known(cc, 1):
                        sp.wait_ge(group_used, val((cc - 1) * NG + NG))
                elif g >= RING:
                    sp.wait_ge(group_used, val(cc * NG + (g - RING + 1)))
                elif known(cc, 1):
                    sp.wait_ge(group_used, val((cc - 1) * NG + (NG - 1 - RING + g + 1)))
                if width(c) == CW:
                    src = adj_main[c, g] if isinstance(c, int) else adj_main[bass.ds(val(c), 1), g].rearrange(
                        "a p n -> (a p) n")
                    sp.dma_start(adjb[:, slot].rearrange("p t w -> p (t w)"), src).then_inc(slot_in[slot], 16)
                else:
                    sp.dma_start(adjb[:, slot, :, 0:LASTW], adj_last[g].rearrange("p (t w) -> p t w", t=GT)
                                 ).then_inc(slot_in[slot], 16)
                if g == 4:
                    w = width(c)
                    sp.dma_start(adjr[:, par, 0:w], adj_rest[:, bass.ds(val(c * CW), w)]).then_inc(rest_in, 16)

            def chunk0(c, par):
                for g in range(NG):
                    load_adj(0, c, g, par)
                    if g == 6 and known(c, 1):
                        store_x1(c - 1, 1 - par)
                    if g == 0:
                        load_x(c, par)

            def store_x1(c, par):
                settled(sp)
                sp.wait_ge(x1_ready, val(c + 1))
                if known(c, 1):
                    sp.wait_ge(x1_stored, val(c * 16))
                w = width(c)
                if w == CW:
                    sp.dma_start(x1_dram[bass.ds(val(c * CW), CW), :].rearrange("(r p) d -> p r d", p=P), x1_s[par]
                                 ).then_inc(x1_stored, 16)
                else:
                    whole = w // P * P
                    sp.dma_start(x1_dram[c * CW:c * CW + whole, :].rearrange("(r p) d -> p r d", p=P),
                                 x1_s[par][:, 0:w // P, :]).then_inc(x1_stored, 16)
                    sp.dma_start(x1_dram[c * CW + whole:NODES, :], x1_s[par][0:w - whole, w // P, :]
                                 ).then_inc(x1_stored, 16)

            chunks0(sp.Fori, chunk0)

            def load_x1(t, par):
                if known(t, 1):
                    sp.wait_ge(out_stored, val(t * 16))
                w = width(t)
                if w == CW:
                    sp.dma_start(x1_in, x1_dram[bass.ds(val(t * CW), CW), :].rearrange("(r p) d -> p r d", p=P)
                                 ).then_inc(x1_back, 16)
                else:
                    whole = w // P * P
                    sp.dma_start(x1_in[:, 0:w // P, :], x1_dram[t * CW:t * CW + whole, :].rearrange(
                        "(r p) d -> p r d", p=P)).then_inc(x1_back, 16)
                    sp.dma_start(x1_in[0:w - whole, w // P, :], x1_dram[t * CW + whole:NODES, :]
                                 ).then_inc(x1_back, 16)

            def store_out(t, par):
                sp.wait_ge(out_ready, val(t + 1))
                w = width(t)
                if w == CW:
                    sp.dma_start(out[bass.ds(val(t * CW), CW), :].rearrange("(r p) d -> p r d", p=P), x1_in
                                 ).then_inc(out_stored, 16)
                else:
                    whole = w // P * P
                    sp.dma_start(out[t * CW:t * CW + whole, :].rearrange("(r p) d -> p r d", p=P),
                                 x1_in[:, 0:w // P, :]).then_inc(out_stored, 16)
                    sp.dma_start(out[t * CW + whole:NODES, :], x1_in[0:w - whole, w // P, :]
                                 ).then_inc(out_stored, 16)

            def one_round(a, f, s, t, par):
                for g in range(NG):
                    if a is not None:
                        load_adj(1, a, g, 1 - par)
                    if t is not None and g == 1:
                        load_x1(t, par)
                    if t is not None and g == 9:
                        store_out(t, par)
                    if f is None and s is None and t is None and g == 5:
                        store_x1(NC - 1, (NC - 1) % 2)
                        sp.wait_ge(x1_stored, (NC + 1) * 16)

            rounds(sp.Fori, one_round)
            sp.wait_ge(out_stored, (NC + 1) * 16)

        @block.gpsimd
        def _(pool):
            nc.gpsimd.memset(ident[:, :], 0.0).then_inc(consts, 1)
            nc.gpsimd.memset(pick[:, :, :], 0.0).then_inc(consts, 1)
            nc.gpsimd.memset(ones[:, :], 1.0).then_inc(consts, 1)
            nc.gpsimd.memset(mean_w[:, :], 1.0 / D).then_inc(consts, 1)
            nc.gpsimd.memset(eps_c[:, :], EPS).then_inc(consts, 1)
            nc.gpsimd.memset(state[:, :, :], 0.0).then_inc(consts, 1)
            nc.gpsimd.memset(w_xp_s[:, :, :], 0.0).then_inc(consts, 1)
            pool.wait_ge(consts, 7)
            nc.gpsimd.affine_select(out=ident[:, :], in_=ident[:, :], compare_op=ALU.not_equal, fill=1.0, base=0,
                                    pattern=[[-1, P]], channel_multiplier=1).then_inc(consts, 1)
            for k in range(3):
                nc.gpsimd.affine_select(out=pick[:, :, :], in_=pick[:, :, :], compare_op=ALU.not_equal, fill=1.0,
                                        base=-32 * (k + 1), pattern=[[-1, 2 * NS], [0, P]],
                                        channel_multiplier=1).then_inc(consts, 1)
                pool.wait_ge(consts, val(9 + k))
            ld = [(gcn_w_s[:, :], gcn_w), (w_in_s[:, :], w_in), (w_dt_s[:, :], w_dt),
                  (w_out_s[:, :, :], w_out.rearrange("(h p) d -> p h d", p=P)),
                  (gcn_b_c[:, :], gcn_b.rearrange("(p a) -> p a", a=1)),
                  (ln_g_c[:, :], ln_g.rearrange("(p a) -> p a", a=1)),
                  (ln_b_c[:, :], ln_b.rearrange("(p a) -> p a", a=1)),
                  (conv_w_c[:, :, :], conv_w.rearrange("(h p) k -> p h k", p=P)),
                  (conv_b_c[:, :], conv_b),
                  (b_dt_c[:, :], b_dt),
                  (skip_c[:, :], D_skip),
                  (A_c[:, :, :], A_log.rearrange("(h p) n -> p h n", p=P))]
            xp = w_xp.rearrange("(h p) n -> p h n", p=P)
            ld += [(w_xp_s[:, :, 0:RANK], xp[:, :, 0:RANK])]
            ld += [(w_xp_s[:, :, 32 * k:32 * k + 2 * NS], xp[:, :, RANK:RANK + 2 * NS]) for k in (1, 2, 3)]
            for dst, src in ld:
                pool.dma_start(dst, src).then_inc(weights1_in, 16)

            def add_up(s, n, par):
                if s is None or n == 0:
                    return
                pool.wait_ge(weighed, val(s * NS + (n + 1)))
                if n > 1:
                    pool.wait_ge(summed, val(s * (NS - 1) + (n - 1)))
                w = width(s)
                y = ysum[par][:, :, 0:w]
                nc.gpsimd.tensor_tensor(y, y, drive[n % 4][:, :, 0:w], ALU.add).then_inc(summed, 1)

            def one_round(a, f, s, t, par):
                for n in range(STEPS):
                    if n == 0:
                        add_up(t, NS - 1, par)
                    else:
                        add_up(s, n - 1, 1 - par)
                    if t is not None and n == 3:
                        pool.wait_ge(skip_added, val(t * 2 + 2))
                        pool.wait_ge(front_pool, val(pool_at(t, "gate")))
                        w = width(t)
                        y = ysum[par][:, :, 0:w]
                        nc.gpsimd.tensor_tensor(y, y, gate[par][:, :, 0:w], ALU.mult).then_inc(gated, 1)
                    if f is None:
                        continue
                    w = width(f)
                    if n == 8:
                        pool.wait_ge(front_act, val(act_at(f, "xsig")))
                        nc.gpsimd.tensor_tensor(u[par][:, :, 0:w], u[par][:, :, 0:w], ta[:, :, 0:w],
                                                ALU.mult).then_inc(front_pool, 1)
                    if n == 11:
                        pool.wait_ge(front_dve, val(dve_at(f, "one_e")))
                        pool.wait_ge(front_act, val(act_at(f, "dln")))
                        nc.gpsimd.tensor_tensor(gh[:, :, 0:w], ta[:, :, 0:w], gh[:, :, 0:w],
                                                ALU.subtract).then_inc(front_pool, 1)
                        pool.wait_ge(front_pool, val(pool_at(f, "lost")))
                        nc.gpsimd.tensor_tensor(tb[:, :, 0:w], tb[:, :, 0:w], gh[:, :, 0:w],
                                                ALU.add).then_inc(front_pool, 1)
                    if n == 12:
                        pool.wait_ge(front_dve, val(dve_at(f, "dt")))
                        if known(f, 2):
                            pool.wait_ge(drive_ready, val((f - 1) * NS))
                        nc.gpsimd.tensor_tensor(dtu[par][:, :, 0:w], dt[par][:, :, 0:w], u[par][:, :, 0:w],
                                                ALU.mult).then_inc(front_pool, 1)
                    if n == 15:
                        pool.wait_ge(front_act, val(act_at(f, "zsig")))
                        nc.gpsimd.tensor_tensor(gate[par][:, :, 0:w], gate[par][:, :, 0:w], ta[:, :, 0:w],
                                                ALU.mult).then_inc(front_pool, 1)

            rounds(pool.Fori, one_round)

        @block.scalar
        def _(act):
            act.wait_ge(consts, CONSTS)
            act.wait_ge(bias_spread, 1)
            nc.scalar.activation(bias_b[:, :, :].rearrange("p a d -> p (a d)"), misc[0][:, 0:2 * D],
                                 ACT.Copy).then_inc(bias_kept, 1)
            act.wait_ge(weights1_in, 16 * 16)
            nc.scalar.activation(A_c[:, :, :], A_c[:, :, :], ACT.Exp).then_inc(a_exp, 1)
            act.wait_ge(a_exp, 1)
            nc.scalar.mul(Aneg_c[:, :, :], A_c[:, :, :], -1.0).then_inc(a_neg, 1)

            def normed(k, w, src, stat, lnv_done, rstd_done, shift_done, count, write):
                np_ = len(row_parts(w))
                act.wait_ge(stat, val(count))
                for rows, a, b in row_parts(w):
                    ins = nc.scalar.activation(lnv[0:rows, k, a:b], moments[0:rows, k, a:b, 1], ACT.Ln,
                                               bias=eps_c[0:rows, :])
                ins.then_inc(lnv_done, 1)
                act.wait_ge(lnv_done, val(count))
                for rows, a, b in row_parts(w):
                    ins = nc.scalar.activation(rstd4[0:rows, k, a:b], lnv[0:rows, k, a:b], ACT.Exp, scale=-0.5)
                ins.then_inc(rstd_done, 1)
                act.wait_ge(rstd_done, val(count))
                act.wait_ge(shift_done, val(count))
                for r, rows in row_tiles(w):
                    ins = nc.scalar.activation(write(r, rows), src[0:rows, r, :], ACT.Relu,
                                               bias=nmr4[0:rows, k, r:r + 1], scale=rstd4[0:rows, k, r:r + 1])
                return ins

            def keep_acc(c, cc, par, dst):
                w = width(c)
                act.wait_ge(acc_full, val(cc + 1))
                return nc.scalar.activation(dst[:, 0:w], acc[par][:, 0:w], ACT.Copy)

            def node_rows(c, par):
                node = node_h[:, :].rearrange("p (t d) -> p t d", d=D)
                if isinstance(c, int):
                    write = lambda r, rows: node[0:rows, c * 4 + r, :]
                else:
                    write = lambda r, rows: node_h[0:rows, bass.ds(val(c * CW + r * D), D)]
                normed(1, width(c), x1_s[par], x1_stat, x1_lnv, x1_rstd, x1_shift, c + 1, write
                       ).then_inc(node_ready, 1)

            def chunk0(c, par):
                w = width(c)
                if known(c, 1):
                    if known(c, 2):
                        act.wait_ge(rows_done, val(c - 1))
                    keep_acc(c - 1, c - 1, 1 - par, aggT).then_inc(acc_read, 1)
                    node_rows(c - 1, 1 - par)
                if known(c, 1):
                    act.wait_ge(userT_done, val(c))
                normed(0, w, x_in[par], user_stat, user_lnv, user_rstd, user_shift, c + 1,
                       lambda r, rows: user_h[0:rows, r, :]).then_inc(user_ready, 1)
                if known(c, 2):
                    act.wait_ge(rows_done, val(c - 1))
                act.wait_ge(userT_done, val(c + 1))
                nc.scalar.activation(userT[par][:, 0:w], misc[1][:, 0:w], ACT.Copy).then_inc(userT_kept, 1)

            chunks0(act.Fori, chunk0)

            def decays(c, m, par):
                if c is None:
                    return
                if m == 0:
                    act.wait_ge(front_dve, val(dve_at(c, "dt")))
                if m >= 2 or known(c, 1):
                    act.wait_ge(scanned, val(c * NS + (m - 1)))
                w = width(c)
                for h in range(HALF):
                    ins = nc.scalar.activation(decay[m % 2][:, h, 0:w], dt[par][:, h, 0:w], ACT.Exp,
                                               scale=Aneg_c[:, h, m:m + 1])
                ins.then_inc(decay_ready, 1)

            def keep_state(c, m):
                if c is None:
                    return
                act.wait_ge(scanned, val(c * NS + (m + 1)))
                w = width(c)
                nc.scalar.activation(state[:, m, :], hist[m % 2][:, :, w - 1], ACT.Copy).then_inc(state_kept, 1)

            def one_round(a, f, s, t, par):
                if f is None and s is None and t is None:
                    act.wait_ge(rows_done, NC - 1)
                    keep_acc(NC - 1, NC - 1, (NC - 1) % 2, aggT).then_inc(acc_read, 1)
                    node_rows(NC - 1, (NC - 1) % 2)
                    return
                for n in range(STEPS):
                    c, m = scan_index(s, f, n + 1)
                    if n + 1 < NS:
                        decays(c, m, 1 - par)
                    c, m = (t, NS - 1) if n == 0 else (s, n - 1)
                    keep_state(c, m)
                    if f is None:
                        continue
                    w = width(f)
                    if n == 0:
                        if known(f, 1):
                            act.wait_ge(front_pool, val(pool_at(f - 1, "log")))
                        keep_acc(f, f + NC, par, g_s).then_inc(acc_read, 1)
                    if n == 1:
                        act.wait_ge(front_pe, val(pe_at(f, "gcn")))
                        nc.scalar.activation(h_s[:, 0:w], misc[0][:, 0:w], ACT.Relu,
                                             bias=gcn_b_c[:, :]).then_inc(front_act, 1)
                    if n == 2:
                        act.wait_ge(front_dve, val(dve_at(f, "centre")))
                        nc.scalar.activation(g_s[:, 0:w], h_s[:, 0:w], ACT.Square).then_inc(front_act, 1)
                    if n == 3:
                        act.wait_ge(front_pe, val(pe_at(f, "var")))
                        nc.scalar.activation(g_s[:, 0:w], misc[0][:, 0:w], ACT.Ln,
                                             bias=eps_c[:, :]).then_inc(front_act, 1)
                        act.wait_ge(front_act, val(act_at(f, "lnvar")))
                        nc.scalar.activation(g_s[:, 0:w], g_s[:, 0:w], ACT.Exp, scale=-0.5).then_inc(front_act, 1)
                    if n == 4:
                        act.wait_ge(front_dve, val(dve_at(f, "scaled")))
                        nc.scalar.activation(h_s[:, 0:w], h_s[:, 0:w], ACT.Identity, bias=ln_b_c[:, :],
                                             scale=ln_g_c[:, :]).then_inc(front_act, 1)
                    if n == 5:
                        for h in range(HALF):
                            act.wait_ge(front_pe, val(pe_at(f, f"xc{h}")))
                            act.wait_ge(conv_tail, val(f + 1))
                            nc.scalar.activation(xc[:, h, TAPS - 1:TAPS - 1 + w], misc[h][:, 0:w],
                                                 ACT.Copy).then_inc(front_act, 1)
                        for h in range(HALF):
                            if known(f, 2):
                                act.wait_ge(skip_added, val((f - 2) * 2 + 2))
                            act.wait_ge(front_act, val(act_at(f, "xc1")))
                            nc.scalar.activation(u[par][:, h, 0:w], xc[:, h, TAPS - 1:TAPS - 1 + w], ACT.Identity,
                                                 bias=conv_b_c[:, h:h + 1],
                                                 scale=conv_w_c[:, h, TAPS - 1:TAPS]).then_inc(front_act, 1)
                    if n == 6:
                        for h in range(HALF):
                            act.wait_ge(front_pe, val(pe_at(f, f"z{h}")))
                            if known(f, 2):
                                act.wait_ge(gated, val(f - 1))
                            nc.scalar.activation(gate[par][:, h, 0:w], misc[h][:, 0:w], ACT.Copy).then_inc(front_act, 1)
                    if n in (7, 13):
                        src, last = (u, "conv5") if n == 7 else (gate, None)
                        x_ = "x" if n == 7 else "z"
                        if last:
                            act.wait_ge(front_dve, val(dve_at(f, last)))
                            if known(f, 1):
                                act.wait_ge(front_pool, val(pool_at(f - 1, "gate")))
                        else:
                            act.wait_ge(front_act, val(act_at(f, "z1")))
                            act.wait_ge(front_pool, val(pool_at(f, "lost")))
                        nc.scalar.activation(ta[:, :, 0:w], src[par][:, :, 0:w], ACT.Abs).then_inc(front_act, 1)
                        act.wait_ge(front_act, val(act_at(f, x_ + "abs")))
                        nc.scalar.activation(ta[:, :, 0:w], ta[:, :, 0:w], ACT.Exp, scale=-1.0).then_inc(front_act, 1)
                        act.wait_ge(front_act, val(act_at(f, x_ + "exp")))
                        nc.scalar.activation(ta[:, :, 0:w], ta[:, :, 0:w], ACT.Ln, bias=1.0).then_inc(front_act, 1)
                    if n in (8, 14):
                        x_ = "x" if n == 8 else "z"
                        act.wait_ge(front_dve, val(dve_at(f, x_ + "min")))
                        nc.scalar.activation(ta[:, :, 0:w], ta[:, :, 0:w], ACT.Exp).then_inc(front_act, 1)
                    if n == 9:
                        act.wait_ge(front_pe, val(pe_at(f, "dbc")))
                        nc.scalar.activation(dtrow[:, 0:w], misc[0][0:RANK, 0:w], ACT.Copy).then_inc(front_act, 1)
                        if known(f, 2):
                            act.wait_ge(c_spread, val((f - 1) * NS))
                        nc.scalar.activation(parts[par][:, 0:w], misc[0][:, 0:w], ACT.Copy).then_inc(front_act, 1)
                        act.wait_ge(front_dve, val(dve_at(f, "bc_rest")))
                        nc.scalar.activation(parts[par][64:128, 0:w], rest_s[64:128, 0:w],
                                             ACT.Copy).then_inc(front_act, 1)
                    if n == 10:
                        for h in range(HALF):
                            act.wait_ge(front_pe, val(pe_at(f, f"dt{h}")))
                            bank_ = misc[1 - h]
                            if h == 0 and known(f, 2):
                                act.wait_ge(front_pool, val(pool_at(f - 2, "dtu")))
                                act.wait_ge(decay_ready, val((f - 1) * NS))
                            nc.scalar.activation(dt[par][:, h, 0:w], bank_[:, 0:w], ACT.Identity,
                                                 bias=b_dt_c[:, h:h + 1]).then_inc(front_act, 1)
                            act.wait_ge(front_pool, val(pool_at(f, "u")))
                            nc.scalar.activation(ta[:, h, 0:w], bank_[:, 0:w], ACT.Abs,
                                                 bias=b_dt_c[:, h:h + 1]).then_inc(front_act, 1)
                        act.wait_ge(front_act, val(act_at(f, "abs1")))
                        nc.scalar.activation(ta[:, :, 0:w], ta[:, :, 0:w], ACT.Exp, scale=-1.0).then_inc(front_act, 1)
                        act.wait_ge(front_act, val(act_at(f, "dexp")))
                        if known(f, 1):
                            act.wait_ge(front_dve, val(dve_at(f - 1, "dt")))
                        nc.scalar.activation(tb[:, :, 0:w], ta[:, :, 0:w], ACT.Ln, bias=1.0).then_inc(front_act, 1)
                    if n == STEPS - 1:
                        decays(f, 0, par)

            rounds(act.Fori, one_round)

        @block.vector
        def _(dve):
            dve.wait_ge(consts, CONSTS)
            dve.wait_ge(bias_kept, 1)
            for k in range(NC):
                tiles = min(4, FULL + 1 - 4 * k)
                dve.wait_ge(item_done, val(k + 1))
                for r in range(0, tiles):
                    rows = P if 4 * k + r < FULL else REST
                    if r == 0 or rows < P:
                        n_ = tiles if (4 * k + tiles <= FULL) else tiles - 1
                        if rows < P:
                            ins = nc.vector.tensor_tensor(item_h[0:rows, FULL * D:(FULL + 1) * D],
                                                          misc[k % 2][0:rows, r * D:(r + 1) * D],
                                                          bias_b[0:rows, 0, :], ALU.add)
                        else:
                            ins = nc.vector.tensor_tensor(
                                item_h[:, 4 * k * D:(4 * k + n_) * D].rearrange("p (r d) -> p r d", d=D),
                                misc[k % 2][:, 0:n_ * D].rearrange("p (r d) -> p r d", d=D),
                                bias_b[:, 0:1, :].broadcast_to([P, n_, D]), ALU.add)
                ins.then_inc(item_kept, 1)

            def stat_ops(k, w, src):
                for r, rows in row_tiles(w):
                    ins = nc.vector.bn_stats(stats[0:rows, k, r, :], src[0:rows, r, :])
                return ins

            def aggr_ops(k, w):
                for r, rows in row_tiles(w):
                    ins = nc.vector.bn_aggr(moments[0:rows, k, r, :], stats[0:rows, k, r, :])
                return ins

            def shift_ops(k, w):
                for rows, a, b in row_parts(w):
                    ins = nc.vector.scalar_tensor_tensor(out=nmr4[0:rows, k, a:b], in0=moments[0:rows, k, a:b, 0],
                                                         scalar=-1.0, in1=rstd4[0:rows, k, a:b],
                                                         op0=ALU.mult, op1=ALU.mult)
                return ins

            def finish_rows(c, par):
                w = width(c)
                dve.wait_ge(rows_done, val(c + 1))
                if known(c, 2):
                    dve.wait_ge(x1_stored, val((c - 1) * 16))
                if known(c, 1):
                    dve.wait_ge(node_ready, val(c))
                m = misc[0][:, :].rearrange("p (r d) -> p r d", d=D)
                for rows, a, b in row_parts(w):
                    ins = nc.vector.tensor_tensor(x1_s[par][0:rows, a:b, :], m[0:rows, a:b, :],
                                                  bias_b[0:rows, 1:2, :].broadcast_to([rows, b - a, D]), ALU.add)
                ins.then_inc(rows_biased, 1)
                dve.wait_ge(rows_biased, val(c + 1))
                for rows, a, b in row_parts(w):
                    ins = nc.vector.scalar_tensor_tensor(out=x1_s[par][0:rows, a:b, :], in0=x1_s[par][0:rows, a:b, :],
                                                         scalar=0.0, in1=x_in[par][0:rows, a:b, :],
                                                         op0=ALU.max, op1=ALU.add)
                ins.then_inc(x1_ready, 1)
                dve.wait_ge(x1_ready, val(c + 1))
                stat_ops(1, w, x1_s[par]).then_inc(x1_bn, 1)
                settled(dve)
                dve.wait_ge(x1_bn, val(c + 1))
                aggr_ops(1, w).then_inc(x1_stat, 1)
                dve.wait_ge(x1_rstd, val(c + 1))
                shift_ops(1, w).then_inc(x1_shift, 1)

            def chunk0(c, par):
                w = width(c)
                if known(c, 1):
                    finish_rows(c - 1, 1 - par)
                dve.wait_ge(x_loaded, val((c + 1) * 16 if w == CW else (c + 2) * 16))
                if known(c, 1):
                    dve.wait_ge(user_ready, val(c))
                stat_ops(0, w, x_in[par]).then_inc(user_bn, 16)
                settled(dve)
                dve.wait_ge(user_bn, val((c + 1) * 16))
                aggr_ops(0, w).then_inc(user_stat, 1)
                dve.wait_ge(user_rstd, val(c + 1))
                shift_ops(0, w).then_inc(user_shift, 1)

            chunks0(dve.Fori, chunk0)

            def drives(c, m, par):
                if c is None:
                    return
                dve.wait_ge(b_spread, val(c * NS + (m + 1)))
                if m == 0:
                    dve.wait_ge(front_pool, val(pool_at(c, "dtu")))
                if m >= 4 or known(c, 1):
                    dve.wait_ge(scanned, val(c * NS + (m - 3)))
                if m >= 5:
                    dve.wait_ge(summed, val(c * (NS - 1) + (m - 4)))
                elif m < 4 and known(c, 1):
                    dve.wait_ge(summed, val((c - 1) * (NS - 1) + (m + 12)))
                w = width(c)
                nc.vector.tensor_tensor(drive[m % 4][:, :, 0:w], dtu[par][:, :, 0:w],
                                        b_all[m % 2][:, None, 0:w].broadcast_to([P, HALF, w]),
                                        ALU.mult).then_inc(drive_ready, 1)

            def scans(c, m):
                if c is None:
                    return
                w = width(c)
                dve.wait_ge(decay_ready, val(c * NS + (m + 1)))
                dve.wait_ge(drive_ready, val(c * NS + (m + 1)))
                if m >= 2 or known(c, 1):
                    dve.wait_ge(weighed, val(c * NS + (m - 1)))
                    dve.wait_ge(state_kept, val(c * NS + (m - 1)))
                for h in range(HALF):
                    ins = nc.vector.tensor_tensor_scan(hist[m % 2][:, h, 0:w], decay[m % 2][:, h, 0:w],
                                                       drive[m % 4][:, h, 0:w], state[:, m, h:h + 1],
                                                       ALU.mult, ALU.add)
                ins.then_inc(scanned, 1)

            def weighs(c, m, par):
                if c is None:
                    return
                w = width(c)
                dve.wait_ge(c_spread, val(c * NS + (m + 1)))
                dve.wait_ge(scanned, val(c * NS + (m + 1)))
                dst = drive[m % 4]
                if m == 0:
                    dst = ysum[par]
                    if known(c, 2):
                        dve.wait_ge(projected, val(c - 1))
                nc.vector.tensor_tensor(dst[:, :, 0:w], hist[m % 2][:, :, 0:w],
                                        c_all[m % 2][:, None, 0:w].broadcast_to([P, HALF, w]),
                                        ALU.mult).then_inc(weighed, 1)

            def one_round(a, f, s, t, par):
                if f is None and s is None and t is None:
                    finish_rows(NC - 1, (NC - 1) % 2)
                    dve.wait_ge(node_ready, NC)
                    nc.vector.memset(xc[:, :, 0:TAPS - 1], 0.0).then_inc(conv_tail, 1)
                    dve.wait_ge(x1_stored, (NC + 1) * 16)
                    return
                for n in range(STEPS):
                    if n + 1 < NS:
                        drives(s, n + 1, 1 - par)
                    scans(s, n)
                    if n == 0:
                        weighs(t, NS - 1, par)
                    else:
                        weighs(s, n - 1, 1 - par)
                    if t is not None and n == 2:
                        w = width(t)
                        dve.wait_ge(summed, val((t + 1) * (NS - 1)))
                        for h in range(HALF):
                            nc.vector.scalar_tensor_tensor(out=ysum[par][:, h, 0:w], in0=u[par][:, h, 0:w],
                                                           scalar=skip_c[:, h:h + 1], in1=ysum[par][:, h, 0:w],
                                                           op0=ALU.mult, op1=ALU.add).then_inc(skip_added, 1)
                    if t is not None and n == 5:
                        w = width(t)
                        dve.wait_ge(projected, val(t + 1))
                        dve.wait_ge(x1_back, val((t + 1) * 16 if w == CW else (t + 2) * 16))
                        m_ = misc[1][:, :].rearrange("p (r d) -> p r d", d=D)
                        for rows, a_, b_ in row_parts(w):
                            ins = nc.vector.tensor_tensor(x1_in[0:rows, a_:b_, :], m_[0:rows, a_:b_, :],
                                                          x1_in[0:rows, a_:b_, :], ALU.add)
                        ins.then_inc(out_ready, 1)
                    if f is None:
                        continue
                    w = width(f)
                    if n == 2:
                        dve.wait_ge(front_pe, val(pe_at(f, "mean")))
                        nc.vector.tensor_tensor(h_s[:, 0:w], h_s[:, 0:w], misc[1][:, 0:w],
                                                ALU.subtract).then_inc(front_dve, 1)
                    if n == 3:
                        dve.wait_ge(front_act, val(act_at(f, "rstd")))
                        nc.vector.tensor_tensor(h_s[:, 0:w], h_s[:, 0:w], g_s[:, 0:w],
                                                ALU.mult).then_inc(front_dve, 1)
                    if n == 6:
                        dve.wait_ge(front_act, val(act_at(f, "tap1")))
                        for k in range(TAPS - 1):
                            for h in range(HALF):
                                j = k * HALF + h
                                if j >= HALF:
                                    dve.wait_ge(front_dve, val(dve_at(f, f"conv{j - HALF}")))
                                nc.vector.scalar_tensor_tensor(
                                    out=u[par][:, h, 0:w], in0=xc[:, h, k:k + w], scalar=conv_w_c[:, h, k:k + 1],
                                    in1=u[par][:, h, 0:w], op0=ALU.mult, op1=ALU.add).then_inc(front_dve, 1)
                        dve.wait_ge(front_dve, val(dve_at(f, "conv5")))
                        nc.vector.tensor_copy(xc[:, :, 0:TAPS - 1], xc[:, :, w:w + TAPS - 1]).then_inc(conv_tail, 1)
                    if n in (8, 14):
                        x_, src = ("x", u) if n == 8 else ("z", gate)
                        dve.wait_ge(front_act, val(act_at(f, x_ + "ln")))
                        nc.vector.scalar_tensor_tensor(out=ta[:, :, 0:w], in0=src[par][:, :, 0:w], scalar=0.0,
                                                       in1=ta[:, :, 0:w], op0=ALU.min,
                                                       op1=ALU.subtract).then_inc(front_dve, 1)
                    if n == 9:
                        dve.wait_ge(front_act, val(act_at(f, "bc_hi")))
                        nc.vector.tensor_tensor(rest_s[64:128, 0:w], misc[0][64:128, 0:w], parts[par][64:128, 0:w],
                                                ALU.subtract).then_inc(front_dve, 1)
                    if n == 10:
                        dve.wait_ge(front_act, val(act_at(f, "bc_mid")))
                        nc.vector.tensor_tensor(parts[par][96:128, 0:w], rest_s[96:128, 0:w], parts[par][96:128, 0:w],
                                                ALU.subtract).then_inc(front_dve, 1)
                        dve.wait_ge(front_act, val(act_at(f, "dexp")))
                        nc.vector.tensor_scalar(gh[:, :, 0:w], ta[:, :, 0:w], 1.0, -1.0, ALU.add,
                                                ALU.add).then_inc(front_dve, 1)
                    if n == 11:
                        dve.wait_ge(front_pool, val(pool_at(f, "log")))
                        nc.vector.scalar_tensor_tensor(out=dt[par][:, :, 0:w], in0=dt[par][:, :, 0:w], scalar=0.0,
                                                       in1=tb[:, :, 0:w], op0=ALU.max,
                                                       op1=ALU.add).then_inc(front_dve, 1)
                    if n == STEPS - 1:
                        drives(f, 0, par)

            rounds(dve.Fori, one_round)

        @block.tensor
        def _(pe):
            pe.wait_ge(consts, CONSTS)
            pe.wait_ge(weights_in, 16 * 4)
            for k in range(2):
                ins = nc.tensor.matmul(misc[0][:, k * D:(k + 1) * D], ones[:, :], bias_rows[:, k, :],
                                       start=True, stop=True)
            ins.then_inc(bias_spread, 1)
            pe.wait_ge(bias_kept, 1)
            for k in range(NC):
                pe.wait_ge(feat_in, val((k // 5 + 1) * 16))
                if k >= 2:
                    pe.wait_ge(item_kept, val(k - 1))
                for t in range(4 * k, min(4 * k + 4, FULL + 1)):
                    rows = P if t < FULL else REST
                    ins = nc.tensor.matmul(misc[k % 2][0:rows, (t % 4) * D:(t % 4 + 1) * D],
                                           node_h[:, t * P:t * P + rows], w_itemT_s[:, :], start=True, stop=True)
                ins.then_inc(item_done, 1)
            pe.wait_ge(item_kept, NC)

            def products(layer, c, par, step):
                cc = c + layer * NC
                w = width(c)
                feats = item_h if layer == 0 else node_h
                if step == 0 and known(cc, 2):
                    pe.wait_ge(acc_read, val(cc - 1))
                for t in range(FULL * step // STEPS, FULL * (step + 1) // STEPS):
                    g, j = divmod(t, GT)
                    slot = g % RING if g < NG - 1 else RING
                    if j == 0:
                        turns = (NG - 1) // RING if slot < RING else 1
                        pe.wait_ge(slot_in[slot], val((cc * turns + (g // RING if slot < RING else 0) + 1) * 16))
                        if layer == 1 and isinstance(c, int) and c == 0:
                            pe.wait_ge(node_ready, val(((g + 1) * GT - 1) // 4 + 1))
                    ins = nc.tensor.matmul(acc[par][:, 0:w], feats[:, t * D:(t + 1) * D], adjb[:, slot, j, 0:w],
                                           start=(t == 0), stop=False)
                    if j == GT - 1:
                        ins.then_inc(group_used, 1)
                if step == STEPS - 1:
                    pe.wait_ge(rest_in, val((cc + 1) * 16))
                    if layer == 1 and isinstance(c, int) and c == 0:
                        pe.wait_ge(node_ready, NC)
                    nc.tensor.matmul(acc[par][:, 0:w], feats[0:REST, FULL * D:(FULL + 1) * D], adjr[:, par, 0:w],
                                     start=False, stop=True).then_inc(acc_full, 1)

            def turn_rows(c, par):
                w = width(c)
                pe.wait_ge(acc_read, val(c + 1))
                pe.wait_ge(userT_kept, val(c + 1))
                if known(c, 1):
                    pe.wait_ge(rows_biased, val(c))
                for r, rows in row_tiles(w):
                    o = misc[0][0:rows, r * D:(r + 1) * D]
                    nc.tensor.matmul(o, aggT[:, r * P:r * P + rows], ident[:, :], start=True, stop=False)
                    ins = nc.tensor.matmul(o, userT[par][:, r * P:r * P + rows], w_userT_s[:, :], start=False,
                                           stop=True)
                ins.then_inc(rows_done, 1)

            def chunk0(c, par):
                w = width(c)
                for step in range(STEPS):
                    products(0, c, par, step)
                    if step == 2 and known(c, 1):
                        turn_rows(c - 1, 1 - par)
                    if step == 10:
                        pe.wait_ge(user_ready, val(c + 1))
                        if known(c, 1):
                            pe.wait_ge(userT_kept, val(c))
                        for r, rows in row_tiles(w):
                            ins = nc.tensor.transpose(misc[1][:, r * P:r * P + rows], user_h[0:rows, r, :],
                                                      ident[0:rows, 0:rows])
                        ins.then_inc(userT_done, 1)

            chunks0(pe.Fori, chunk0)

            def spread(c, m, dst, sel, par, done):
                w = width(c)
                nc.tensor.matmul(dst[m % 2][:, 0:w], pick[:, sel + m, :], parts[par][:, 0:w], start=True,
                                 stop=True).then_inc(done, 1)

            def one_round(a, f, s, t, par):
                for n in range(STEPS):
                    if s is not None:
                        if n >= 2 or known(s, 1):
                            pe.wait_ge(weighed, val(s * NS + (n - 1)))
                        spread(s, n, c_all, NS, 1 - par, c_spread)
                    c, m = scan_index(s, f, n + 2)
                    if c is not None and not (n + 2 >= NS and f is None):
                        if m == 0:
                            pe.wait_ge(front_dve, val(dve_at(c, "bc_low")))
                        if m >= 2 or known(c, 1):
                            pe.wait_ge(drive_ready, val(c * NS + (m - 1)))
                        spread(c, m, b_all, 0, par if n + 2 >= NS else 1 - par, b_spread)
                    if t is not None and n == 4:
                        w = width(t)
                        pe.wait_ge(gated, val(t + 1))
                        for r, rows in row_tiles(w):
                            for h in range(HALF):
                                ins = nc.tensor.matmul(misc[1][0:rows, r * D:(r + 1) * D],
                                                       ysum[par][:, h, r * P:r * P + rows], w_out_s[:, h, :],
                                                       start=(h == 0), stop=(h == HALF - 1))
                        ins.then_inc(projected, 1)
                    if f is not None:
                        w = width(f)
                        if n == 1:
                            if not known(f, 1):
                                pe.wait_ge(weights1_in, 16 * 16)
                            pe.wait_ge(acc_read, val(f + NC + 1))
                            if known(f, 1):
                                pe.wait_ge(front_act, val(act_at(f - 1, "abs1")))
                            else:
                                pe.wait_ge(rows_biased, NC)
                            nc.tensor.matmul(misc[0][:, 0:w], gcn_w_s[:, :], g_s[:, 0:w], start=True,
                                             stop=True).then_inc(front_pe, 1)
                        if n == 2:
                            pe.wait_ge(front_act, val(act_at(f, "h")))
                            nc.tensor.matmul(misc[1][:, 0:w], mean_w[:, :], h_s[:, 0:w], start=True,
                                             stop=True).then_inc(front_pe, 1)
                        if n == 3:
                            pe.wait_ge(front_act, val(act_at(f, "square")))
                            nc.tensor.matmul(misc[0][:, 0:w], mean_w[:, :], g_s[:, 0:w], start=True,
                                             stop=True).then_inc(front_pe, 1)
                        if n == 5:
                            pe.wait_ge(front_act, val(act_at(f, "norm")))
                            if known(f, 2):
                                pe.wait_ge(out_ready, val(f - 1))
                            for h in range(HALF):
                                nc.tensor.matmul(misc[h][:, 0:w], w_in_s[:, h * P:(h + 1) * P], h_s[:, 0:w],
                                                 start=True, stop=True).then_inc(front_pe, 1)
                        if n == 6:
                            for h in range(HALF):
                                pe.wait_ge(front_act, val(act_at(f, f"xc{h}")))
                                nc.tensor.matmul(misc[h][:, 0:w], w_in_s[:, DI + h * P:DI + (h + 1) * P],
                                                 h_s[:, 0:w], start=True, stop=True).then_inc(front_pe, 1)
                        if n == 9:
                            pe.wait_ge(front_pool, val(pool_at(f, "u")))
                            pe.wait_ge(front_act, val(act_at(f, "z1")))
                            for h in range(HALF):
                                ins = nc.tensor.matmul(misc[0][:, 0:w], w_xp_s[:, h, :], u[par][:, h, 0:w],
                                                       start=(h == 0), stop=(h == HALF - 1))
                            ins.then_inc(front_pe, 1)
                        if n == 10:
                            pe.wait_ge(front_act, val(act_at(f, "dtrow")))
                            for h in range(HALF):
                                if h == 1:
                                    pe.wait_ge(front_dve, val(dve_at(f, "bc_rest")))
                                nc.tensor.matmul(misc[1 - h][:, 0:w], w_dt_s[:, h * P:(h + 1) * P],
                                                 dtrow[:, 0:w], start=True, stop=True).then_inc(front_pe, 1)
                    if a is not None:
                        products(1, a, 1 - par, n)
                    if f is None and s is None and t is None and n == 2:
                        turn_rows(NC - 1, (NC - 1) % 2)

            rounds(pe.Fori, one_round)


_INS = ["adj_main", "adj_last", "adj_rest", "x", "featT", "w_itemT", "b_item", "w_userT", "b_user", "gcn_w", "gcn_b",
        "ln_g", "ln_b", "w_in", "conv_w", "conv_b", "w_xp", "w_dt", "b_dt", "A_log", "D_skip", "w_out"]


def laid_out(inputs):
    import numpy as np
    got = {k.split("_gnn_")[-1] if k[0] == "L" else k: np.asarray(v) for k, v in inputs.items()}
    adjT = got["adj"].T
    top = FULL * P
    whole = (NC - 1) * CW
    return {
        "adj_main": np.ascontiguousarray(
            adjT[:top, :whole].reshape(NG, GT, P, NC - 1, CW).transpose(3, 0, 2, 1, 4)).reshape(NC - 1, NG, P, GT * CW),
        "adj_last": np.ascontiguousarray(
            adjT[:top, whole:].reshape(NG, GT, P, LASTW).transpose(0, 2, 1, 3)).reshape(NG, P, GT * LASTW),
        "adj_rest": np.ascontiguousarray(adjT[top:]),
        "x": got["x"],
        "featT": np.ascontiguousarray(got["item_feat"].T),
        "w_itemT": np.ascontiguousarray(got["W_item"].T),
        "w_userT": np.ascontiguousarray(got["W_user"].T),
        **{k: np.ascontiguousarray(got[k].reshape(HALF, P).T) for k in ("conv_b", "b_dt", "D_skip")},
        **{k: np.ascontiguousarray(got[k]) for k in ("b_item", "b_user", "gcn_w", "gcn_b", "ln_g", "ln_b", "w_in",
                                                     "conv_w", "w_xp", "w_dt", "A_log", "w_out")},
    }


def kernel(**inputs):
    import concourse.bacc as bacc
    from concourse.bass_utils import run_bass_kernel_spmd

    nc = bacc.Bacc("TRN2", target_bir_lowering=False, num_devices=1)
    arrays = laid_out(inputs)
    args = [nc.dram_tensor(f"in_{k}", arrays[k].shape, F32, kind="ExternalInput").ap() for k in _INS]
    out = nc.dram_tensor("out_rows", (NODES, D), F32, kind="ExternalOutput").ap()
    gnn_mamba(nc, *args, out)
    r = run_bass_kernel_spmd(nc, [{f"in_{k}": arrays[k] for k in _INS}], core_ids=[0])
    return r.results[0]["out_rows"]
```

```python
from contextlib import ExitStack

import concourse.bass as bass
from concourse import mybir

ALU = mybir.AluOpType
ACT = mybir.ActivationFunctionType
F32 = mybir.dt.float32
BF16 = mybir.dt.bfloat16
F32R = mybir.dt.float32r

CONSTS = 7
P = 128
D = 128
NODES = 10000
CW = 512
NC = -(-NODES // CW)
LASTW = NODES - (NC - 1) * CW
FULL = NODES // P
REST = NODES - FULL * P
GT = 3
NG = FULL // GT
RING = 5
FEAT_LOADS = 4
SPLIT = 6
STEPS = 16
NS = 16
DI = 256
HALF = DI // P
RANK = 8
TAPS = 4
EPS = 1e-5

FRONT_ACT = ["h", "square", "lnvar", "rstd", "norm", "norm_hi", "xc0", "xc1", "tap0", "tap1", "z0", "z1",
             "xabs", "xexp", "xln", "xsig", "dt_signed", "bc_hi", "bc_mid",
             "raw0", "abs0", "raw1", "abs1", "dexp", "dln", "zabs", "zexp", "zln", "zsig"]
FRONT_DVE = ["centre", "scaled", "norm_lo", "conv0", "conv1", "conv2", "conv3", "conv4", "conv5", "xmin",
             "dt_pair", "bc_rest", "bc_low", "one_e", "dt", "zmin"]
FRONT_POOL = ["u", "lost", "log", "dtu", "gate"]
FRONT_PE = ["gcn", "mean", "var", "xc0", "xc1", "z0", "z1", "dbc", "dt0", "dt1"]


class Count:

    def __init__(self, i, a, b):
        self.i, self.a, self.b = i, a, b

    def __add__(self, n):
        return Count(self.i, self.a, self.b + n)

    def __sub__(self, n):
        return Count(self.i, self.a, self.b - n)

    def __mul__(self, n):
        return Count(self.i, self.a * n, self.b * n)


def val(c):
    if isinstance(c, Count):
        assert c.b > 0, "a wait that isn't above zero in the first turn"
        return c.i * c.a + c.b if c.b else c.i * c.a
    return c


def act_at(c, name):
    return c * len(FRONT_ACT) + FRONT_ACT.index(name) + 1


def dve_at(c, name):
    return c * len(FRONT_DVE) + FRONT_DVE.index(name) + 1


def pool_at(c, name):
    return c * len(FRONT_POOL) + FRONT_POOL.index(name) + 1


def pe_at(c, name):
    return c * len(FRONT_PE) + FRONT_PE.index(name) + 1


def known(c, least):
    return c is not None and (not isinstance(c, int) or c >= least)


def row_tiles(w):
    return [(r, min(P, w - r * P)) for r in range(-(-w // P))]


def row_parts(w):
    whole, rest = divmod(w, P)
    return [(P, 0, whole)] + ([(rest, whole, whole + 1)] if rest else [])


def gnn_mamba(nc, adj_main, adj_last, adj_rest, x, featT, w_itemT, b_item, w_userT, b_user,
              gcn_w, gcn_b, ln_g, ln_b, w_in, conv_w, conv_b, w_xp, w_dt4, dt_rule, b_dt, A_log, D_skip, w_out, out):
    with ExitStack() as ctx:
        sbuf_start = nc.sbuf_base

        def sem(name):
            return ctx.enter_context(nc.semaphore(name))

        x1_dram = nc.dram_tensor("x1_dram", (NODES, D), F32, kind="Internal").ap()

        ctx.enter_context(nc.sbuf_tensor("all_sbuf", [P, (nc.sbuf_usable_end - nc.sbuf_base) // 4 - 32], F32))
        top = {"both": -(-sbuf_start // 32) * 32}

        def place(where, name, shape, dt=F32):
            size = 2 if dt == BF16 else 4
            for n in shape[1:]:
                size *= n
            t = nc.alloc_sbuf_tensor_at(name, shape, dt, offset=top[where])
            top[where] += -(-size // 32) * 32
            assert top[where] <= nc.sbuf_usable_end, (name, top[where] - nc.sbuf_usable_end)
            return t

        def both(name, shape, dt=F32):
            return place("both", name, shape, dt)

        adjb = both("adjb", [P, RING + 1, GT, CW])
        adjr = both("adjr", [REST, 2, CW])
        node_h = both("node_h", [P, (FULL + 1) * D])
        ident = both("ident", [P, P])
        mean_w = both("mean_w", [P, P])
        gcn_w_s = both("gcn_w_s", [P, D])
        w_in_hi = both("w_in_hi", [P, 2 * DI], F32R)
        w_in_lo = both("w_in_lo", [P, 2 * DI], F32R)
        w_xp_s = both("w_xp_s", [P, HALF, P])
        w_dt_pair = both("w_dt_pair", [4 * RANK, DI], F32R)
        w_out_s = both("w_out_s", [P, HALF, D])
        ones = both("ones", [1, P])
        eps_c = both("eps_c", [P, 1])
        dt_rule_c = both("dt_rule_c", [4 * RANK, 4])
        gcn_b_c = both("gcn_b_c", [P, 1])
        ln_g_c = both("ln_g_c", [P, 1])
        ln_b_c = both("ln_b_c", [P, 1])
        conv_w_c = both("conv_w_c", [P, HALF, TAPS])
        conv_b_c = both("conv_b_c", [P, HALF])
        b_dt_c = both("b_dt_c", [P, HALF])
        skip_c = both("skip_c", [P, HALF])
        A_c = both("A_c", [P, HALF, NS])
        Aneg_c = both("Aneg_c", [P, HALF, NS])
        state = both("state", [P, NS, HALF])
        stats = both("stats", [P, 2, 4, 6])
        moments = both("moments", [P, 2, 4, 2])
        lnv = both("lnv", [P, 2, 4])
        rstd4 = both("rstd4", [P, 2, 4])
        nmr4 = both("nmr4", [P, 2, 4])
        top["layer0"] = top["layer1"] = top["both"]

        item_hi = place("layer0", "item_hi", [P, FULL * D], F32R)
        item_lo = place("layer0", "item_lo", [P, FULL * D], F32R)
        adj_hi = place("layer0", "adj_hi", [P, SPLIT, CW], F32R)
        adj_lo = place("layer0", "adj_lo", [P, SPLIT, CW], F32R)
        item_rest = place("layer0", "item_rest", [REST, D])

        def rows4(name):
            return place("layer0", name, [P, CW])

        x_in = [rows4(f"x_in{k}")[:, :].rearrange("p (r d) -> p r d", d=D) for k in range(2)]
        user_w, agg_w, userT, x1_w = rows4("user_h"), rows4("aggT"), rows4("userT"), rows4("x1_s")
        user_h = user_w[:, :].rearrange("p (r d) -> p r d", d=D)
        x1_s = x1_w[:, :].rearrange("p (r d) -> p r d", d=D)
        aggT = agg_w[:, :]
        item_raw = [agg_w, x1_w]
        w_in_raw = user_w
        small_raw = userT
        w_itemT_s = place("layer0", "w_itemT_s", [P, D])
        w_userT_s = place("layer0", "w_userT_s", [P, D])
        bias_b = place("layer0", "bias_b", [P, 2, D])

        def pair(name):
            return place("layer1", name, [P, HALF, CW])

        pick = place("layer1", "pick", [P, 2 * NS, P], BF16)
        u = [pair(f"u{k}") for k in range(2)]
        dt = [pair(f"dt{k}") for k in range(2)]
        dtu = [pair(f"dtu{k}") for k in range(2)]
        gate = [pair(f"gate{k}") for k in range(2)]
        ta, tb, gh = pair("ta"), pair("tb"), pair("gh")
        g_s, h_s = gh[:, 0, :], gh[:, 1, :]
        norm_hi = place("layer1", "norm_hi", [P, CW], F32R)
        norm_lo = place("layer1", "norm_lo", [P, CW], F32R)
        parts = [place("layer1", f"parts{k}", [P, CW], BF16) for k in range(2)]
        rest_s = place("layer1", "rest_s", [P, CW])
        dt_pair = place("layer1", "dt_pair", [4 * RANK, CW], F32R)
        x1_in = place("layer1", "x1_in", [P, CW])[:, :].rearrange("p (r d) -> p r d", d=D)
        xc = place("layer1", "xc", [P, HALF, CW + TAPS - 1])
        decay = [pair(f"decay{k}") for k in range(2)]
        drive = [pair(f"drive{k}") for k in range(4)]
        hist = [pair(f"hist{k}") for k in range(2)]
        ysum = [pair(f"ysum{k}") for k in range(2)]

        def bank(name):
            return ctx.enter_context(nc.psum_tensor(name, [P, CW], F32))

        acc = [bank(f"acc{i}") for i in range(2)]
        misc = [bank(f"misc{i}") for i in range(2)]
        b_all = [bank(f"b_all{i}") for i in range(2)]
        c_all = [bank(f"c_all{i}") for i in range(2)]

        feat_in = [sem(f"feat_in{k}") for k in range(FEAT_LOADS)]
        weights_in = sem("weights_in")
        weights1_in = sem("weights1_in")
        consts = sem("consts")
        bias_spread = sem("bias_spread")
        bias_kept = sem("bias_kept")
        item_done = sem("item_done")
        item_kept = sem("item_kept")
        item_split = sem("item_split")
        slot_in = [sem(f"adj_in{i}") for i in range(RING + 1)]
        rest_in = sem("rest_in")
        group_used = sem("group_used")
        tile_used = sem("tile_used")
        adj_hi_ready = sem("adj_hi_ready")
        adj_split = sem("adj_split")
        item_hi_ready = sem("item_hi_ready")
        item_rest_ready = sem("item_rest_ready")
        w_in_raw_in = sem("w_in_raw_in")
        weights_hi = sem("weights_hi")
        weights_lo = sem("weights_lo")
        pick_cleared = sem("pick_cleared")
        pick_ready = sem("pick_ready")
        acc_full = sem("acc_full")
        acc_read = sem("acc_read")
        x_loaded = sem("x_loaded")
        user_bn = sem("user_bn")
        x1_bn = sem("x1_bn")
        user_stat = sem("user_stat")
        user_lnv = sem("user_lnv")
        user_rstd = sem("user_rstd")
        user_shift = sem("user_shift")
        user_ready = sem("user_ready")
        userT_done = sem("userT_done")
        userT_kept = sem("userT_kept")
        rows_done = sem("rows_done")
        rows_biased = sem("rows_biased")
        x1_ready = sem("x1_ready")
        x1_stat = sem("x1_stat")
        x1_lnv = sem("x1_lnv")
        x1_rstd = sem("x1_rstd")
        x1_shift = sem("x1_shift")
        node_ready = sem("node_ready")
        x1_stored = sem("x1_stored")
        a_exp = sem("a_exp")
        a_neg = sem("a_neg")
        front_act = sem("front_act")
        front_dve = sem("front_dve")
        front_pool = sem("front_pool")
        front_pe = sem("front_pe")
        conv_tail = sem("conv_tail")
        b_spread = sem("b_spread")
        c_spread = sem("c_spread")
        decay_ready = sem("decay_ready")
        drive_ready = sem("drive_ready")
        scanned = sem("scanned")
        state_kept = sem("state_kept")
        weighed = sem("weighed")
        summed = sem("summed")
        skip_added = sem("skip_added")
        gated = sem("gated")
        projected = sem("projected")
        out_ready = sem("out_ready")
        x1_back = sem("x1_back")
        out_stored = sem("out_stored")

        block = ctx.enter_context(nc.Block())

        dt_signed_w = x_in[1].rearrange("p r d -> p (r d)")[0:4 * RANK, 0:DI]

        def width(c):
            return LASTW if isinstance(c, int) and c == NC - 1 else CW

        def slot_of(g):
            return (g % RING, g // RING) if g < NG - 1 else (RING, 0)

        TURNS = [(NG - 1) // RING] * RING + [1]

        def rounds(fori, one_round):
            def at(f):
                one_round(*[k if 0 <= k < NC else None for k in (f + 1, f, f - 1, f - 2)], f % 2)

            for f in range(-1, 4):
                at(f)
            with fori(0, (NC - 6) // 2) as i:
                for k in range(2):
                    one_round(Count(i, 2, 5 + k), Count(i, 2, 4 + k), Count(i, 2, 3 + k), Count(i, 2, 2 + k), k)
            for f in range(NC - 2, NC + 2):
                at(f)

        def chunks0(fori, one_chunk):
            for c in range(3):
                one_chunk(c, c % 2)
            with fori(0, (NC - 4) // 2) as i:
                one_chunk(Count(i, 2, 3), 1)
                one_chunk(Count(i, 2, 4), 0)
            one_chunk(NC - 1, (NC - 1) % 2)

        item_banks = b_all + c_all

        def items_at(g, all_so_far):
            return [k for k in range(NC) if (4 * k // GT <= g if all_so_far else 4 * k // GT == g)]

        def scan_index(s, f, n):
            return (s, n) if n < NS else (f, n - NS)

        def settled(engine):
            engine.wait_ge(consts, CONSTS)

        @block.sync
        def _(sp):
            def load_feat(k):
                cut = NC // FEAT_LOADS * 4 * P
                e = min((k + 1) * cut, NODES)
                sp.dma_start(node_h[:, k * cut:e], featT[:, k * cut:e]).then_inc(feat_in[k], 16)

            sp.dma_start(w_itemT_s[:, :], w_itemT).then_inc(weights_in, 16)
            load_feat(0)
            sp.dma_start(small_raw[0:1, DI:DI + D], b_item.rearrange("(a n) -> a n", a=1)).then_inc(weights_in, 16)
            sp.dma_start(small_raw[0:1, DI + D:DI + 2 * D], b_user.rearrange("(a n) -> a n", a=1)).then_inc(weights_in, 16)
            sp.dma_start(w_userT_s[:, :], w_userT).then_inc(weights_in, 16)
            sp.dma_start(small_raw[0:4 * RANK, 0:DI], w_dt4).then_inc(weights_in, 16)
            sp.dma_start(dt_rule_c[:, :], dt_rule).then_inc(weights_in, 16)
            sp.dma_start(w_in_raw[:, :], w_in).then_inc(w_in_raw_in, 16)

            def load_x(c, par):
                settled(sp)
                if known(c, 2):
                    sp.wait_ge(x1_ready, val(c - 1))
                if known(c, 1):
                    sp.wait_ge(x_loaded, val(c * 16))
                w = width(c)
                if w == CW:
                    sp.dma_start(x_in[par], x[bass.ds(val(c * CW), CW), :].rearrange("(r p) d -> p r d", p=P)
                                 ).then_inc(x_loaded, 16)
                else:
                    whole = w // P * P
                    sp.dma_start(x_in[par][:, 0:w // P, :], x[c * CW:c * CW + whole, :].rearrange(
                        "(r p) d -> p r d", p=P)).then_inc(x_loaded, 16)
                    sp.dma_start(x_in[par][0:w - whole, w // P, :], x[c * CW + whole:NODES, :]
                                 ).then_inc(x_loaded, 16)

            def load_adj(layer, c, g, par):
                cc = c + layer * NC
                slot = g % RING if g < NG - 1 else RING
                back = c if g >= RING and g < NG - 1 else c - 1
                last = NG if g == NG - 1 else g - RING + 1 if g >= RING else NG - 1 - RING + g + 1
                if isinstance(back, int) and back < 0:
                    if layer == 1:
                        sp.wait_ge(adj_split, (NC - 1) * FULL + last * GT)
                elif layer == 0:
                    sp.wait_ge(adj_split, val(back * FULL + last * GT))
                else:
                    sp.wait_ge(group_used, val(back * NG + last))
                if width(c) == CW:
                    src = adj_main[c, g] if isinstance(c, int) else adj_main[bass.ds(val(c), 1), g].rearrange(
                        "a p n -> (a p) n")
                    sp.dma_start(adjb[:, slot].rearrange("p t w -> p (t w)"), src).then_inc(slot_in[slot], 16)
                else:
                    sp.dma_start(adjb[:, slot, :, 0:LASTW], adj_last[g].rearrange("p (t w) -> p t w", t=GT)
                                 ).then_inc(slot_in[slot], 16)
                if g == 8:
                    w = width(c)
                    sp.dma_start(adjr[:, par, 0:w], adj_rest[:, bass.ds(val(c * CW), w)]).then_inc(rest_in, 16)

            def chunk0(c, par):
                for g in range(NG):
                    if not known(c, 1) and g in (1, 6, 13):
                        load_feat((0, 1, 6, 13).index(g))
                    load_adj(0, c, g, par)
                    if g == 18 and known(c, 1):
                        store_x1(c - 1)
                    if g == 0:
                        load_x(c, par)

            def store_x1(c):
                settled(sp)
                sp.wait_ge(x1_ready, val(c + 1))
                if known(c, 1):
                    sp.wait_ge(x1_stored, val(c * 16))
                w = width(c)
                if w == CW:
                    sp.dma_start(x1_dram[bass.ds(val(c * CW), CW), :].rearrange("(r p) d -> p r d", p=P), x1_s
                                 ).then_inc(x1_stored, 16)
                else:
                    whole = w // P * P
                    sp.dma_start(x1_dram[c * CW:c * CW + whole, :].rearrange("(r p) d -> p r d", p=P),
                                 x1_s[:, 0:w // P, :]).then_inc(x1_stored, 16)
                    sp.dma_start(x1_dram[c * CW + whole:NODES, :], x1_s[0:w - whole, w // P, :]
                                 ).then_inc(x1_stored, 16)

            chunks0(sp.Fori, chunk0)

            def load_x1(t, par):
                if known(t, 1):
                    sp.wait_ge(out_stored, val(t * 16))
                w = width(t)
                if w == CW:
                    sp.dma_start(x1_in, x1_dram[bass.ds(val(t * CW), CW), :].rearrange("(r p) d -> p r d", p=P)
                                 ).then_inc(x1_back, 16)
                else:
                    whole = w // P * P
                    sp.dma_start(x1_in[:, 0:w // P, :], x1_dram[t * CW:t * CW + whole, :].rearrange(
                        "(r p) d -> p r d", p=P)).then_inc(x1_back, 16)
                    sp.dma_start(x1_in[0:w - whole, w // P, :], x1_dram[t * CW + whole:NODES, :]
                                 ).then_inc(x1_back, 16)

            def store_out(t, par):
                sp.wait_ge(out_ready, val(t + 1))
                w = width(t)
                if w == CW:
                    sp.dma_start(out[bass.ds(val(t * CW), CW), :].rearrange("(r p) d -> p r d", p=P), x1_in
                                 ).then_inc(out_stored, 16)
                else:
                    whole = w // P * P
                    sp.dma_start(out[t * CW:t * CW + whole, :].rearrange("(r p) d -> p r d", p=P),
                                 x1_in[:, 0:w // P, :]).then_inc(out_stored, 16)
                    sp.dma_start(out[t * CW + whole:NODES, :], x1_in[0:w - whole, w // P, :]
                                 ).then_inc(out_stored, 16)

            def one_round(a, f, s, t, par):
                for g in range(NG):
                    if a is not None:
                        load_adj(1, a, g, 1 - par)
                    if t is not None and g == 2:
                        load_x1(t, par)
                    if t is not None and g == 18:
                        store_out(t, par)
                    if f is None and s is None and t is None and g == 16:
                        store_x1(NC - 1)
                        sp.wait_ge(x1_stored, (NC + 1) * 16)

            rounds(sp.Fori, one_round)
            sp.wait_ge(out_stored, (NC + 1) * 16)

        @block.gpsimd
        def _(pool):
            nc.gpsimd.memset(ident[:, :], 0.0).then_inc(consts, 1)
            nc.gpsimd.memset(ones[:, :], 1.0).then_inc(consts, 1)
            nc.gpsimd.memset(mean_w[:, :], 1.0 / D).then_inc(consts, 1)
            nc.gpsimd.memset(eps_c[:, :], EPS).then_inc(consts, 1)
            nc.gpsimd.memset(state[:, :, :], 0.0).then_inc(consts, 1)
            nc.gpsimd.memset(w_xp_s[:, :, :], 0.0).then_inc(consts, 1)
            pool.wait_ge(consts, 6)
            nc.gpsimd.affine_select(out=ident[:, :], in_=ident[:, :], compare_op=ALU.not_equal, fill=1.0, base=0,
                                    pattern=[[-1, P]], channel_multiplier=1).then_inc(consts, 1)
            for k in range(NC):
                n_ = min(4, FULL - 4 * k)
                at_ = slice(4 * k * D, (4 * k + n_) * D)
                pool.wait_ge(item_hi_ready, k + 1)
                nc.gpsimd.tensor_tensor(item_lo[:, at_], item_raw[k % 2][:, 0:n_ * D], item_hi[:, at_].bitcast(F32),
                                        ALU.subtract).then_inc(item_split, 1)

            ld = [(gcn_w_s[:, :], gcn_w),
                  (w_out_s[:, :, :], w_out.rearrange("(h p) d -> p h d", p=P)),
                  (gcn_b_c[:, :], gcn_b.rearrange("(p a) -> p a", a=1)),
                  (ln_g_c[:, :], ln_g.rearrange("(p a) -> p a", a=1)),
                  (ln_b_c[:, :], ln_b.rearrange("(p a) -> p a", a=1)),
                  (conv_w_c[:, :, :], conv_w.rearrange("(h p) k -> p h k", p=P)),
                  (conv_b_c[:, :], conv_b),
                  (b_dt_c[:, :], b_dt),
                  (skip_c[:, :], D_skip),
                  (A_c[:, :, :], A_log.rearrange("(h p) n -> p h n", p=P))]
            xp = w_xp.rearrange("(h p) n -> p h n", p=P)
            ld += [(w_xp_s[:, :, RANK * k:RANK * (k + 1)], xp[:, :, 0:RANK]) for k in range(4)]
            ld += [(w_xp_s[:, :, 32 * k:32 * k + 2 * NS], xp[:, :, RANK:RANK + 2 * NS]) for k in (1, 2, 3)]
            for dst, src in ld:
                pool.dma_start(dst, src).then_inc(weights1_in, 16)

            def add_up(s, n, par):
                if s is None or n == 0:
                    return
                pool.wait_ge(weighed, val(s * NS + (n + 1)))
                if n > 1:
                    pool.wait_ge(summed, val(s * (NS - 1) + (n - 1)))
                w = width(s)
                y = ysum[par][:, :, 0:w]
                nc.gpsimd.tensor_tensor(y, y, drive[n % 4][:, :, 0:w], ALU.add).then_inc(summed, 1)

            def one_round(a, f, s, t, par):
                if f is None and s is None and t is None:
                    pool.wait_ge(acc_full, NC)
                    nc.gpsimd.memset(pick[:, :, :], 0.0).then_inc(pick_cleared, 1)
                    for k in range(3):
                        pool.wait_ge(pick_cleared, k + 1)
                        nc.gpsimd.affine_select(out=pick[:, :, :], in_=pick[:, :, :], compare_op=ALU.not_equal,
                                                fill=1.0, base=-32 * (k + 1), pattern=[[-1, 2 * NS], [0, P]],
                                                channel_multiplier=1).then_inc(pick_cleared if k < 2 else pick_ready, 1)
                for n in range(STEPS):
                    if n == 0:
                        add_up(t, NS - 1, par)
                    elif f is None or n not in (9, 12, 14):
                        add_up(s, n - 1, 1 - par)
                    if t is not None and n == 3:
                        pool.wait_ge(skip_added, val(t * 2 + 2))
                        pool.wait_ge(front_pool, val(pool_at(t, "gate")))
                        w = width(t)
                        y = ysum[par][:, :, 0:w]
                        nc.gpsimd.tensor_tensor(y, y, gate[par][:, :, 0:w], ALU.mult).then_inc(gated, 1)
                    if f is None:
                        continue
                    w = width(f)
                    if n == 9:
                        pool.wait_ge(front_act, val(act_at(f, "xsig")))
                        nc.gpsimd.tensor_tensor(u[par][:, :, 0:w], u[par][:, :, 0:w], ta[:, :, 0:w],
                                                ALU.mult).then_inc(front_pool, 1)
                        add_up(s, n - 1, 1 - par)
                    if n == 12:
                        pool.wait_ge(front_dve, val(dve_at(f, "one_e")))
                        pool.wait_ge(front_act, val(act_at(f, "dln")))
                        nc.gpsimd.tensor_tensor(gh[:, :, 0:w], ta[:, :, 0:w], gh[:, :, 0:w],
                                                ALU.subtract).then_inc(front_pool, 1)
                        pool.wait_ge(front_pool, val(pool_at(f, "lost")))
                        nc.gpsimd.tensor_tensor(tb[:, :, 0:w], tb[:, :, 0:w], gh[:, :, 0:w],
                                                ALU.add).then_inc(front_pool, 1)
                        add_up(s, n - 1, 1 - par)
                    if n == 14:
                        pool.wait_ge(front_dve, val(dve_at(f, "dt")))
                        if known(f, 2):
                            pool.wait_ge(drive_ready, val((f - 1) * NS))
                        nc.gpsimd.tensor_tensor(dtu[par][:, :, 0:w], dt[par][:, :, 0:w], u[par][:, :, 0:w],
                                                ALU.mult).then_inc(front_pool, 1)
                        add_up(s, n - 1, 1 - par)
                    if n == 15:
                        pool.wait_ge(front_act, val(act_at(f, "zsig")))
                        nc.gpsimd.tensor_tensor(gate[par][:, :, 0:w], gate[par][:, :, 0:w], ta[:, :, 0:w],
                                                ALU.mult).then_inc(front_pool, 1)

            rounds(pool.Fori, one_round)

        @block.scalar
        def _(act):
            act.wait_ge(consts, CONSTS)
            act.wait_ge(bias_spread, 1)
            nc.scalar.activation(bias_b[:, :, :].rearrange("p a d -> p (a d)"), misc[0][:, 0:2 * D],
                                 ACT.Copy).then_inc(bias_kept, 1)
            act.wait_ge(w_in_raw_in, 16)
            nc.scalar.activation(w_in_hi[:, :], w_in_raw[:, :], ACT.Copy).then_inc(weights_hi, 1)
            nc.scalar.activation(dt_signed_w, small_raw[0:4 * RANK, 0:DI], ACT.Identity,
                                 scale=dt_rule_c[:, 3:4]).then_inc(weights_hi, 1)

            def item_part1(k):
                n_ = min(4, FULL - 4 * k)
                act.wait_ge(item_kept, k + 1)
                nc.scalar.activation(item_hi[:, 4 * k * D:(4 * k + n_) * D], item_raw[k % 2][:, 0:n_ * D],
                                     ACT.Copy).then_inc(item_hi_ready, 1)

            def take_lnv(k, w, stat, count):
                act.wait_ge(stat, val(count))
                for rows, a, b in row_parts(w):
                    ins = nc.scalar.activation(lnv[0:rows, k, a:b], moments[0:rows, k, a:b, 1], ACT.Ln,
                                               bias=eps_c[0:rows, :])
                return ins

            def take_rstd(k, w, lnv_done, count):
                act.wait_ge(lnv_done, val(count))
                for rows, a, b in row_parts(w):
                    ins = nc.scalar.activation(rstd4[0:rows, k, a:b], lnv[0:rows, k, a:b], ACT.Exp, scale=-0.5)
                return ins

            def normed(k, w, src, shift_done, count, write):
                act.wait_ge(shift_done, val(count))
                for r, rows in row_tiles(w):
                    ins = nc.scalar.activation(write(r, rows), src[0:rows, r, :], ACT.Relu,
                                               bias=nmr4[0:rows, k, r:r + 1], scale=rstd4[0:rows, k, r:r + 1])
                return ins

            def keep_acc(c, cc, par, dst):
                w = width(c)
                act.wait_ge(acc_full, val(cc + 1))
                return nc.scalar.activation(dst[:, 0:w], acc[par][:, 0:w], ACT.Copy)

            def node_rows(c):
                node = node_h[:, :].rearrange("p (t d) -> p t d", d=D)
                if isinstance(c, int):
                    write = lambda r, rows: node[0:rows, c * 4 + r, :]
                else:
                    write = lambda r, rows: node_h[0:rows, bass.ds(val(c * CW + r * D), D)]
                normed(1, width(c), x1_s, x1_shift, c + 1, write).then_inc(node_ready, 1)

            def split_hi(c, g, w):
                slot, turn = slot_of(g)
                act.wait_ge(slot_in[slot], val((c * TURNS[slot] + turn + 1) * 16))
                for j in range(GT):
                    t = g * GT + j
                    if t >= SPLIT or known(c, 1):
                        act.wait_ge(tile_used, val(c * FULL + t - SPLIT + 1))
                    nc.scalar.activation(adj_hi[:, t % SPLIT, 0:w], adjb[:, slot, j, 0:w], ACT.Copy
                                         ).then_inc(adj_hi_ready, 1)

            def chunk0(c, par):
                w = width(c)
                for g in range(NG):
                    if not known(c, 1):
                        for k in items_at(g + 1, g == 0):
                            item_part1(k)
                    split_hi(c, g, w)
                    if known(c, 1) and g == 3:
                        if known(c, 2):
                            act.wait_ge(rows_done, val(c - 1))
                        keep_acc(c - 1, c - 1, 1 - par, aggT).then_inc(acc_read, 1)
                    if g == 5:
                        take_lnv(0, w, user_stat, c + 1).then_inc(user_lnv, 1)
                    if g == 6:
                        take_rstd(0, w, user_lnv, c + 1).then_inc(user_rstd, 1)
                    if g == 10:
                        if known(c, 1):
                            act.wait_ge(userT_done, val(c))
                        normed(0, w, x_in[par], user_shift, c + 1,
                               lambda r, rows: user_h[0:rows, r, :]).then_inc(user_ready, 1)
                    if known(c, 1) and g == 14:
                        take_lnv(1, width(c - 1), x1_stat, c).then_inc(x1_lnv, 1)
                    if known(c, 1) and g == 15:
                        take_rstd(1, width(c - 1), x1_lnv, c).then_inc(x1_rstd, 1)
                    if g == 17:
                        if known(c, 1):
                            act.wait_ge(rows_done, val(c))
                        act.wait_ge(userT_done, val(c + 1))
                        nc.scalar.activation(userT[:, 0:w], misc[1][:, 0:w], ACT.Copy).then_inc(userT_kept, 1)
                    if known(c, 1) and g == 19:
                        node_rows(c - 1)

            chunks0(act.Fori, chunk0)

            act.wait_ge(weights1_in, 16 * 17)
            nc.scalar.activation(A_c[:, :, :], A_c[:, :, :], ACT.Exp).then_inc(a_exp, 1)
            act.wait_ge(a_exp, 1)
            nc.scalar.mul(Aneg_c[:, :, :], A_c[:, :, :], -1.0).then_inc(a_neg, 1)

            def decays(c, m, par):
                if c is None:
                    return
                if m == 0:
                    act.wait_ge(front_dve, val(dve_at(c, "dt")))
                if m >= 2 or known(c, 1):
                    act.wait_ge(scanned, val(c * NS + (m - 1)))
                w = width(c)
                for h in range(HALF):
                    ins = nc.scalar.activation(decay[m % 2][:, h, 0:w], dt[par][:, h, 0:w], ACT.Exp,
                                               scale=Aneg_c[:, h, m:m + 1])
                ins.then_inc(decay_ready, 1)

            def keep_state(c, m):
                if c is None:
                    return
                act.wait_ge(scanned, val(c * NS + (m + 1)))
                w = width(c)
                nc.scalar.activation(state[:, m, :], hist[m % 2][:, :, w - 1], ACT.Copy).then_inc(state_kept, 1)

            def one_round(a, f, s, t, par):
                if f is None and s is None and t is None:
                    act.wait_ge(rows_done, NC - 1)
                    keep_acc(NC - 1, NC - 1, (NC - 1) % 2, aggT).then_inc(acc_read, 1)
                    take_lnv(1, LASTW, x1_stat, NC).then_inc(x1_lnv, 1)
                    take_rstd(1, LASTW, x1_lnv, NC).then_inc(x1_rstd, 1)
                    node_rows(NC - 1)
                    return
                for n in range(STEPS):
                    c, m = scan_index(s, f, n + 1)
                    if n + 1 < NS:
                        decays(c, m, 1 - par)
                    c, m = (t, NS - 1) if n == 0 else (s, n - 1)
                    keep_state(c, m)
                    if f is None:
                        continue
                    w = width(f)
                    if n == 0:
                        if known(f, 1):
                            act.wait_ge(front_pool, val(pool_at(f - 1, "log")))
                        keep_acc(f, f + NC, par, g_s).then_inc(acc_read, 1)
                    if n == 1:
                        act.wait_ge(front_pe, val(pe_at(f, "gcn")))
                        nc.scalar.activation(h_s[:, 0:w], misc[0][:, 0:w], ACT.Relu,
                                             bias=gcn_b_c[:, :]).then_inc(front_act, 1)
                    if n == 2:
                        act.wait_ge(front_dve, val(dve_at(f, "centre")))
                        nc.scalar.activation(g_s[:, 0:w], h_s[:, 0:w], ACT.Square).then_inc(front_act, 1)
                    if n == 3:
                        act.wait_ge(front_pe, val(pe_at(f, "var")))
                        nc.scalar.activation(g_s[:, 0:w], misc[0][:, 0:w], ACT.Ln,
                                             bias=eps_c[:, :]).then_inc(front_act, 1)
                        act.wait_ge(front_act, val(act_at(f, "lnvar")))
                        nc.scalar.activation(g_s[:, 0:w], g_s[:, 0:w], ACT.Exp, scale=-0.5).then_inc(front_act, 1)
                    if n == 5:
                        act.wait_ge(front_dve, val(dve_at(f, "scaled")))
                        nc.scalar.activation(h_s[:, 0:w], h_s[:, 0:w], ACT.Identity, bias=ln_b_c[:, :],
                                             scale=ln_g_c[:, :]).then_inc(front_act, 1)
                        act.wait_ge(front_act, val(act_at(f, "norm")))
                        nc.scalar.activation(norm_hi[:, 0:w], h_s[:, 0:w], ACT.Copy).then_inc(front_act, 1)
                    if n == 6:
                        for h in range(HALF):
                            act.wait_ge(front_pe, val(pe_at(f, f"xc{h}")))
                            act.wait_ge(conv_tail, val(f + 1))
                            nc.scalar.activation(xc[:, h, TAPS - 1:TAPS - 1 + w], misc[h][:, 0:w],
                                                 ACT.Copy).then_inc(front_act, 1)
                        for h in range(HALF):
                            if known(f, 2):
                                act.wait_ge(skip_added, val((f - 2) * 2 + 2))
                            act.wait_ge(front_act, val(act_at(f, "xc1")))
                            nc.scalar.activation(u[par][:, h, 0:w], xc[:, h, TAPS - 1:TAPS - 1 + w], ACT.Identity,
                                                 bias=conv_b_c[:, h:h + 1],
                                                 scale=conv_w_c[:, h, TAPS - 1:TAPS]).then_inc(front_act, 1)
                    if n == 7:
                        for h in range(HALF):
                            act.wait_ge(front_pe, val(pe_at(f, f"z{h}")))
                            if known(f, 2):
                                act.wait_ge(gated, val(f - 1))
                            nc.scalar.activation(gate[par][:, h, 0:w], misc[h][:, 0:w], ACT.Copy).then_inc(front_act, 1)
                    if n in (8, 14):
                        src, last = (u, "conv5") if n == 8 else (gate, None)
                        x_ = "x" if n == 8 else "z"
                        if last:
                            act.wait_ge(front_dve, val(dve_at(f, last)))
                            if known(f, 1):
                                act.wait_ge(front_pool, val(pool_at(f - 1, "gate")))
                        else:
                            act.wait_ge(front_act, val(act_at(f, "z1")))
                            act.wait_ge(front_pool, val(pool_at(f, "lost")))
                        nc.scalar.activation(ta[:, :, 0:w], src[par][:, :, 0:w], ACT.Abs).then_inc(front_act, 1)
                        act.wait_ge(front_act, val(act_at(f, x_ + "abs")))
                        nc.scalar.activation(ta[:, :, 0:w], ta[:, :, 0:w], ACT.Exp, scale=-1.0).then_inc(front_act, 1)
                        act.wait_ge(front_act, val(act_at(f, x_ + "exp")))
                        nc.scalar.activation(ta[:, :, 0:w], ta[:, :, 0:w], ACT.Ln, bias=1.0).then_inc(front_act, 1)
                    if n in (9, 15):
                        x_ = "x" if n == 9 else "z"
                        act.wait_ge(front_dve, val(dve_at(f, x_ + "min")))
                        nc.scalar.activation(ta[:, :, 0:w], ta[:, :, 0:w], ACT.Exp).then_inc(front_act, 1)
                    if n == 10:
                        act.wait_ge(front_pe, val(pe_at(f, "dbc")))
                        nc.scalar.activation(rest_s[0:4 * RANK, 0:w].bitcast(F32R), misc[0][0:4 * RANK, 0:w],
                                             ACT.Identity, scale=dt_rule_c[:, 1:2]).then_inc(front_act, 1)
                        if known(f, 2):
                            act.wait_ge(c_spread, val((f - 1) * NS))
                        nc.scalar.activation(parts[par][:, 0:w], misc[0][:, 0:w], ACT.Copy).then_inc(front_act, 1)
                        act.wait_ge(front_dve, val(dve_at(f, "bc_rest")))
                        nc.scalar.activation(parts[par][64:128, 0:w], rest_s[64:128, 0:w],
                                             ACT.Copy).then_inc(front_act, 1)
                    if n == 11:
                        for h in range(HALF):
                            act.wait_ge(front_pe, val(pe_at(f, f"dt{h}")))
                            bank_ = misc[1 - h]
                            if h == 0 and known(f, 2):
                                act.wait_ge(front_pool, val(pool_at(f - 2, "dtu")))
                                act.wait_ge(decay_ready, val((f - 1) * NS))
                            nc.scalar.activation(dt[par][:, h, 0:w], bank_[:, 0:w], ACT.Identity,
                                                 bias=b_dt_c[:, h:h + 1]).then_inc(front_act, 1)
                            act.wait_ge(front_pool, val(pool_at(f, "u")))
                            nc.scalar.activation(ta[:, h, 0:w], bank_[:, 0:w], ACT.Abs,
                                                 bias=b_dt_c[:, h:h + 1]).then_inc(front_act, 1)
                        act.wait_ge(front_act, val(act_at(f, "abs1")))
                        nc.scalar.activation(ta[:, :, 0:w], ta[:, :, 0:w], ACT.Exp, scale=-1.0).then_inc(front_act, 1)
                        act.wait_ge(front_act, val(act_at(f, "dexp")))
                        if known(f, 1):
                            act.wait_ge(front_dve, val(dve_at(f - 1, "dt")))
                        nc.scalar.activation(tb[:, :, 0:w], ta[:, :, 0:w], ACT.Ln, bias=1.0).then_inc(front_act, 1)
                    if n == STEPS - 1:
                        decays(f, 0, par)

            rounds(act.Fori, one_round)

        @block.vector
        def _(dve):
            dve.wait_ge(consts, CONSTS)
            dve.wait_ge(bias_kept, 1)
            dve.wait_ge(weights_hi, 2)
            nc.vector.tensor_tensor(w_in_lo[:, :], w_in_raw[:, :], w_in_hi[:, :].bitcast(F32),
                                    ALU.subtract).then_inc(weights_lo, 1)
            nc.vector.scalar_tensor_tensor(out=w_dt_pair[:, :], in0=small_raw[0:4 * RANK, 0:DI],
                                           scalar=dt_rule_c[:, 2:3], in1=dt_signed_w,
                                           op0=ALU.mult, op1=ALU.add).then_inc(weights_lo, 1)

            def item_bias(k):
                n_ = min(4, FULL - 4 * k)
                bank_ = item_banks[k % 4]
                dve.wait_ge(item_done, k + 1)
                if k >= 2:
                    dve.wait_ge(item_split, k - 1)
                nc.vector.tensor_tensor(
                    item_raw[k % 2][:, 0:n_ * D].rearrange("p (r d) -> p r d", d=D),
                    bank_[:, 0:n_ * D].rearrange("p (r d) -> p r d", d=D),
                    bias_b[:, 0:1, :].broadcast_to([P, n_, D]), ALU.add).then_inc(item_kept, 1)
                if k == NC - 1:
                    nc.vector.tensor_tensor(item_rest[:, :], bank_[0:REST, n_ * D:(n_ + 1) * D],
                                            bias_b[0:REST, 0, :], ALU.add).then_inc(item_rest_ready, 1)

            def stat_ops(k, w, src):
                for r, rows in row_tiles(w):
                    ins = nc.vector.bn_stats(stats[0:rows, k, r, :], src[0:rows, r, :])
                return ins

            def aggr_ops(k, w):
                for r, rows in row_tiles(w):
                    ins = nc.vector.bn_aggr(moments[0:rows, k, r, :], stats[0:rows, k, r, :])
                return ins

            def shift_ops(k, w):
                for rows, a, b in row_parts(w):
                    ins = nc.vector.scalar_tensor_tensor(out=nmr4[0:rows, k, a:b], in0=moments[0:rows, k, a:b, 0],
                                                         scalar=-1.0, in1=rstd4[0:rows, k, a:b],
                                                         op0=ALU.mult, op1=ALU.mult)
                return ins

            def rows_bias(c):
                dve.wait_ge(rows_done, val(c + 1))
                if known(c, 1):
                    dve.wait_ge(x1_stored, val(c * 16))
                    dve.wait_ge(node_ready, val(c))
                m = misc[0][:, :].rearrange("p (r d) -> p r d", d=D)
                for rows, a, b in row_parts(width(c)):
                    ins = nc.vector.tensor_tensor(x1_s[0:rows, a:b, :], m[0:rows, a:b, :],
                                                  bias_b[0:rows, 1:2, :].broadcast_to([rows, b - a, D]), ALU.add)
                ins.then_inc(rows_biased, 1)

            def rows_x1(c, par):
                dve.wait_ge(rows_biased, val(c + 1))
                for rows, a, b in row_parts(width(c)):
                    ins = nc.vector.scalar_tensor_tensor(out=x1_s[0:rows, a:b, :], in0=x1_s[0:rows, a:b, :],
                                                         scalar=0.0, in1=x_in[par][0:rows, a:b, :],
                                                         op0=ALU.max, op1=ALU.add)
                ins.then_inc(x1_ready, 1)

            def rows_stats(c):
                dve.wait_ge(x1_ready, val(c + 1))
                stat_ops(1, width(c), x1_s).then_inc(x1_bn, 1)

            def rows_moments(c):
                settled(dve)
                dve.wait_ge(x1_bn, val(c + 1))
                aggr_ops(1, width(c)).then_inc(x1_stat, 1)

            def rows_shift(c):
                dve.wait_ge(x1_rstd, val(c + 1))
                shift_ops(1, width(c)).then_inc(x1_shift, 1)

            def split_lo(c, g, w):
                slot, _ = slot_of(g)
                for j in range(GT):
                    t = g * GT + j
                    dve.wait_ge(adj_hi_ready, val(c * FULL + t + 1))
                    nc.vector.tensor_tensor(adj_lo[:, t % SPLIT, 0:w], adjb[:, slot, j, 0:w],
                                            adj_hi[:, t % SPLIT, 0:w].bitcast(F32), ALU.subtract
                                            ).then_inc(adj_split, 1)

            def chunk0(c, par):
                w = width(c)
                for g in range(NG):
                    if not known(c, 1):
                        for k in items_at(g + 2, g == 0):
                            item_bias(k)
                    split_lo(c, g, w)
                    if g == 1:
                        dve.wait_ge(x_loaded, val((c + 1) * 16 if w == CW else (c + 2) * 16))
                        if known(c, 1):
                            dve.wait_ge(user_ready, val(c))
                        stat_ops(0, w, x_in[par]).then_inc(user_bn, 16)
                    if g == 2:
                        settled(dve)
                        dve.wait_ge(user_bn, val((c + 1) * 16))
                        aggr_ops(0, w).then_inc(user_stat, 1)
                    if g == 8:
                        dve.wait_ge(user_rstd, val(c + 1))
                        shift_ops(0, w).then_inc(user_shift, 1)
                    if known(c, 1):
                        if g == 9:
                            rows_bias(c - 1)
                        if g == 10:
                            rows_x1(c - 1, 1 - par)
                        if g == 11:
                            rows_stats(c - 1)
                        if g == 12:
                            rows_moments(c - 1)
                        if g == 17:
                            rows_shift(c - 1)

            chunks0(dve.Fori, chunk0)

            def drives(c, m, par):
                if c is None:
                    return
                dve.wait_ge(b_spread, val(c * NS + (m + 1)))
                if m == 0:
                    dve.wait_ge(front_pool, val(pool_at(c, "dtu")))
                if m >= 4 or known(c, 1):
                    dve.wait_ge(scanned, val(c * NS + (m - 3)))
                if m >= 5:
                    dve.wait_ge(summed, val(c * (NS - 1) + (m - 4)))
                elif m < 4 and known(c, 1):
                    dve.wait_ge(summed, val((c - 1) * (NS - 1) + (m + 12)))
                w = width(c)
                nc.vector.tensor_tensor(drive[m % 4][:, :, 0:w], dtu[par][:, :, 0:w],
                                        b_all[m % 2][:, None, 0:w].broadcast_to([P, HALF, w]),
                                        ALU.mult).then_inc(drive_ready, 1)

            def scans(c, m):
                if c is None:
                    return
                w = width(c)
                dve.wait_ge(decay_ready, val(c * NS + (m + 1)))
                dve.wait_ge(drive_ready, val(c * NS + (m + 1)))
                if m >= 2 or known(c, 1):
                    dve.wait_ge(weighed, val(c * NS + (m - 1)))
                    dve.wait_ge(state_kept, val(c * NS + (m - 1)))
                for h in range(HALF):
                    ins = nc.vector.tensor_tensor_scan(hist[m % 2][:, h, 0:w], decay[m % 2][:, h, 0:w],
                                                       drive[m % 4][:, h, 0:w], state[:, m, h:h + 1],
                                                       ALU.mult, ALU.add)
                ins.then_inc(scanned, 1)

            def weighs(c, m, par):
                if c is None:
                    return
                w = width(c)
                dve.wait_ge(c_spread, val(c * NS + (m + 1)))
                dve.wait_ge(scanned, val(c * NS + (m + 1)))
                dst = drive[m % 4]
                if m == 0:
                    dst = ysum[par]
                    if known(c, 2):
                        dve.wait_ge(projected, val(c - 1))
                nc.vector.tensor_tensor(dst[:, :, 0:w], hist[m % 2][:, :, 0:w],
                                        c_all[m % 2][:, None, 0:w].broadcast_to([P, HALF, w]),
                                        ALU.mult).then_inc(weighed, 1)

            def one_round(a, f, s, t, par):
                if f is None and s is None and t is None:
                    rows_bias(NC - 1)
                    rows_x1(NC - 1, (NC - 1) % 2)
                    rows_stats(NC - 1)
                    rows_moments(NC - 1)
                    rows_shift(NC - 1)
                    dve.wait_ge(node_ready, NC)
                    nc.vector.memset(xc[:, :, 0:TAPS - 1], 0.0).then_inc(conv_tail, 1)
                    dve.wait_ge(x1_stored, (NC + 1) * 16)
                    return
                for n in range(STEPS):
                    if n + 1 < NS:
                        drives(s, n + 1, 1 - par)
                    scans(s, n)
                    if n == 0:
                        weighs(t, NS - 1, par)
                    else:
                        weighs(s, n - 1, 1 - par)
                    if t is not None and n == 2:
                        w = width(t)
                        dve.wait_ge(summed, val((t + 1) * (NS - 1)))
                        for h in range(HALF):
                            nc.vector.scalar_tensor_tensor(out=ysum[par][:, h, 0:w], in0=u[par][:, h, 0:w],
                                                           scalar=skip_c[:, h:h + 1], in1=ysum[par][:, h, 0:w],
                                                           op0=ALU.mult, op1=ALU.add).then_inc(skip_added, 1)
                    if t is not None and n == 5:
                        w = width(t)
                        dve.wait_ge(projected, val(t + 1))
                        dve.wait_ge(x1_back, val((t + 1) * 16 if w == CW else (t + 2) * 16))
                        m_ = misc[1][:, :].rearrange("p (r d) -> p r d", d=D)
                        for rows, a_, b_ in row_parts(w):
                            ins = nc.vector.tensor_tensor(x1_in[0:rows, a_:b_, :], m_[0:rows, a_:b_, :],
                                                          x1_in[0:rows, a_:b_, :], ALU.add)
                        ins.then_inc(out_ready, 1)
                    if f is None:
                        continue
                    w = width(f)
                    if n == 2:
                        dve.wait_ge(front_pe, val(pe_at(f, "mean")))
                        nc.vector.tensor_tensor(h_s[:, 0:w], h_s[:, 0:w], misc[1][:, 0:w],
                                                ALU.subtract).then_inc(front_dve, 1)
                    if n == 4:
                        dve.wait_ge(front_act, val(act_at(f, "rstd")))
                        nc.vector.tensor_tensor(h_s[:, 0:w], h_s[:, 0:w], g_s[:, 0:w],
                                                ALU.mult).then_inc(front_dve, 1)
                    if n == 5:
                        dve.wait_ge(front_act, val(act_at(f, "norm_hi")))
                        nc.vector.tensor_tensor(norm_lo[:, 0:w], h_s[:, 0:w], norm_hi[:, 0:w].bitcast(F32),
                                                ALU.subtract).then_inc(front_dve, 1)
                    if n == 7:
                        dve.wait_ge(front_act, val(act_at(f, "tap1")))
                        for k in range(TAPS - 1):
                            for h in range(HALF):
                                j = k * HALF + h
                                if j >= HALF:
                                    dve.wait_ge(front_dve, val(dve_at(f, f"conv{j - HALF}")))
                                nc.vector.scalar_tensor_tensor(
                                    out=u[par][:, h, 0:w], in0=xc[:, h, k:k + w], scalar=conv_w_c[:, h, k:k + 1],
                                    in1=u[par][:, h, 0:w], op0=ALU.mult, op1=ALU.add).then_inc(front_dve, 1)
                        dve.wait_ge(front_dve, val(dve_at(f, "conv5")))
                        nc.vector.tensor_copy(xc[:, :, 0:TAPS - 1], xc[:, :, w:w + TAPS - 1]).then_inc(conv_tail, 1)
                    if n in (9, 15):
                        x_, src = ("x", u) if n == 9 else ("z", gate)
                        dve.wait_ge(front_act, val(act_at(f, x_ + "ln")))
                        nc.vector.scalar_tensor_tensor(out=ta[:, :, 0:w], in0=src[par][:, :, 0:w], scalar=0.0,
                                                       in1=ta[:, :, 0:w], op0=ALU.min,
                                                       op1=ALU.subtract).then_inc(front_dve, 1)
                    if n == 10:
                        dve.wait_ge(front_act, val(act_at(f, "bc_hi")))
                        nc.vector.scalar_tensor_tensor(out=dt_pair[:, 0:w], in0=misc[0][0:4 * RANK, 0:w],
                                                       scalar=dt_rule_c[:, 0:1], in1=rest_s[0:4 * RANK, 0:w],
                                                       op0=ALU.mult, op1=ALU.add).then_inc(front_dve, 1)
                        nc.vector.tensor_tensor(rest_s[64:128, 0:w], misc[0][64:128, 0:w], parts[par][64:128, 0:w],
                                                ALU.subtract).then_inc(front_dve, 1)
                    if n == 11:
                        dve.wait_ge(front_act, val(act_at(f, "bc_mid")))
                        nc.vector.tensor_tensor(parts[par][96:128, 0:w], rest_s[96:128, 0:w], parts[par][96:128, 0:w],
                                                ALU.subtract).then_inc(front_dve, 1)
                        dve.wait_ge(front_act, val(act_at(f, "dexp")))
                        nc.vector.tensor_scalar(gh[:, :, 0:w], ta[:, :, 0:w], 1.0, -1.0, ALU.add,
                                                ALU.add).then_inc(front_dve, 1)
                    if n == 13:
                        dve.wait_ge(front_pool, val(pool_at(f, "log")))
                        nc.vector.scalar_tensor_tensor(out=dt[par][:, :, 0:w], in0=dt[par][:, :, 0:w], scalar=0.0,
                                                       in1=tb[:, :, 0:w], op0=ALU.max,
                                                       op1=ALU.add).then_inc(front_dve, 1)
                    if n == STEPS - 1:
                        drives(f, 0, par)

            rounds(dve.Fori, one_round)

        @block.tensor
        def _(pe):
            pe.wait_ge(consts, CONSTS)
            pe.wait_ge(weights_in, 16 * 6)
            for k in range(2):
                ins = nc.tensor.matmul(misc[0][:, k * D:(k + 1) * D], ones[:, :],
                                       small_raw[0:1, DI + k * D:DI + (k + 1) * D],
                                       start=True, stop=True)
            ins.then_inc(bias_spread, 1)
            pe.wait_ge(bias_kept, 1)

            def item_products(k):
                pe.wait_ge(feat_in[k // (NC // FEAT_LOADS)], 16)
                if k >= 4:
                    pe.wait_ge(item_kept, k - 3)
                for t in range(4 * k, min(4 * k + 4, FULL + 1)):
                    rows = P if t < FULL else REST
                    ins = nc.tensor.matmul(item_banks[k % 4][0:rows, (t % 4) * D:(t % 4 + 1) * D],
                                           node_h[:, t * P:t * P + rows], w_itemT_s[:, :], start=True, stop=True)
                ins.then_inc(item_done, 1)

            for k in range(3):
                item_products(k)

            def products(layer, c, par, step):
                cc = c + layer * NC
                w = width(c)
                if step == 0 and known(cc, 2):
                    pe.wait_ge(acc_read, val(cc - 1))
                for t in range(FULL * step // STEPS, FULL * (step + 1) // STEPS):
                    g, j = divmod(t, GT)
                    slot, turn = slot_of(g)
                    cols = slice(t * D, (t + 1) * D)
                    if layer == 0:
                        if isinstance(c, int) and c == 0 and t % 4 == 0:
                            if t // 4 + 3 < NC:
                                item_products(t // 4 + 3)
                            pe.wait_ge(item_split, t // 4 + 1)
                        pe.wait_ge(adj_split, val(cc * FULL + t + 1))
                        hi, lo = adj_hi[:, t % SPLIT, 0:w], adj_lo[:, t % SPLIT, 0:w]
                        nc.tensor.matmul(acc[par][:, 0:w], item_lo[:, cols], hi, start=(t == 0), stop=False)
                        nc.tensor.matmul(acc[par][:, 0:w], item_hi[:, cols], lo, start=False, stop=False)
                        ins = nc.tensor.matmul(acc[par][:, 0:w], item_hi[:, cols], hi, start=False, stop=False)
                        ins.then_inc(tile_used, 1)
                    else:
                        if j == 0:
                            pe.wait_ge(slot_in[slot], val((cc * TURNS[slot] + turn + 1) * 16))
                            if isinstance(c, int) and c == 0:
                                pe.wait_ge(node_ready, ((g + 1) * GT - 1) // 4 + 1)
                        ins = nc.tensor.matmul(acc[par][:, 0:w], node_h[:, cols], adjb[:, slot, j, 0:w],
                                               start=(t == 0), stop=False)
                        if j == GT - 1:
                            ins.then_inc(group_used, 1)
                if step == STEPS - 1:
                    if layer == 0 and isinstance(c, int) and c == 0:
                        pe.wait_ge(item_rest_ready, 1)
                    pe.wait_ge(rest_in, val((cc + 1) * 16))
                    if layer == 1 and isinstance(c, int) and c == 0:
                        pe.wait_ge(node_ready, NC)
                    rest = item_rest[:, :] if layer == 0 else node_h[0:REST, FULL * D:(FULL + 1) * D]
                    nc.tensor.matmul(acc[par][:, 0:w], rest, adjr[:, par, 0:w],
                                     start=False, stop=True).then_inc(acc_full, 1)

            def turn_rows(c, par):
                w = width(c)
                pe.wait_ge(acc_read, val(c + 1))
                pe.wait_ge(userT_kept, val(c + 1))
                if known(c, 1):
                    pe.wait_ge(rows_biased, val(c))
                for r, rows in row_tiles(w):
                    o = misc[0][0:rows, r * D:(r + 1) * D]
                    nc.tensor.matmul(o, aggT[:, r * P:r * P + rows], ident[:, :], start=True, stop=False)
                    ins = nc.tensor.matmul(o, userT[:, r * P:r * P + rows], w_userT_s[:, :], start=False,
                                           stop=True)
                ins.then_inc(rows_done, 1)

            def chunk0(c, par):
                w = width(c)
                for step in range(STEPS):
                    products(0, c, par, step)
                    if step == 3 and known(c, 1):
                        turn_rows(c - 1, 1 - par)
                    if step == 8:
                        pe.wait_ge(user_ready, val(c + 1))
                        if known(c, 1):
                            pe.wait_ge(userT_kept, val(c))
                        for r, rows in row_tiles(w):
                            ins = nc.tensor.transpose(misc[1][:, r * P:r * P + rows], user_h[0:rows, r, :],
                                                      ident[0:rows, 0:rows])
                        ins.then_inc(userT_done, 1)

            chunks0(pe.Fori, chunk0)

            def in_product(q, w):
                o, cols = misc[q % HALF][:, 0:w], slice(q * P, (q + 1) * P)
                nc.tensor.matmul(o, w_in_lo[:, cols], norm_hi[:, 0:w], start=True, stop=False)
                nc.tensor.matmul(o, w_in_hi[:, cols], norm_lo[:, 0:w], start=False, stop=False)
                return nc.tensor.matmul(o, w_in_hi[:, cols], norm_hi[:, 0:w], start=False, stop=True)

            def spread(c, m, dst, sel, par, done):
                w = width(c)
                nc.tensor.matmul(dst[m % 2][:, 0:w], pick[:, sel + m, :], parts[par][:, 0:w], start=True,
                                 stop=True).then_inc(done, 1)

            def one_round(a, f, s, t, par):
                for n in range(STEPS):
                    if s is not None:
                        if n >= 2 or known(s, 1):
                            pe.wait_ge(weighed, val(s * NS + (n - 1)))
                        spread(s, n, c_all, NS, 1 - par, c_spread)
                    c, m = scan_index(s, f, n + 2)
                    if c is not None and not (n + 2 >= NS and f is None):
                        if m == 0:
                            pe.wait_ge(front_dve, val(dve_at(c, "bc_low")))
                            if not known(c, 1):
                                pe.wait_ge(pick_ready, 1)
                        if m >= 2 or known(c, 1):
                            pe.wait_ge(drive_ready, val(c * NS + (m - 1)))
                        spread(c, m, b_all, 0, par if n + 2 >= NS else 1 - par, b_spread)
                    if t is not None and n == 4:
                        w = width(t)
                        pe.wait_ge(gated, val(t + 1))
                        for r, rows in row_tiles(w):
                            for h in range(HALF):
                                ins = nc.tensor.matmul(misc[1][0:rows, r * D:(r + 1) * D],
                                                       ysum[par][:, h, r * P:r * P + rows], w_out_s[:, h, :],
                                                       start=(h == 0), stop=(h == HALF - 1))
                        ins.then_inc(projected, 1)
                    if f is not None:
                        w = width(f)
                        if n == 1:
                            if not known(f, 1):
                                pe.wait_ge(weights1_in, 16 * 17)
                            pe.wait_ge(acc_read, val(f + NC + 1))
                            if known(f, 1):
                                pe.wait_ge(front_act, val(act_at(f - 1, "abs1")))
                            else:
                                pe.wait_ge(rows_biased, NC)
                            nc.tensor.matmul(misc[0][:, 0:w], gcn_w_s[:, :], g_s[:, 0:w], start=True,
                                             stop=True).then_inc(front_pe, 1)
                        if n == 2:
                            pe.wait_ge(front_act, val(act_at(f, "h")))
                            nc.tensor.matmul(misc[1][:, 0:w], mean_w[:, :], h_s[:, 0:w], start=True,
                                             stop=True).then_inc(front_pe, 1)
                        if n == 3:
                            pe.wait_ge(front_act, val(act_at(f, "square")))
                            nc.tensor.matmul(misc[0][:, 0:w], mean_w[:, :], g_s[:, 0:w], start=True,
                                             stop=True).then_inc(front_pe, 1)
                        if n == 6:
                            pe.wait_ge(front_dve, val(dve_at(f, "norm_lo")))
                            if known(f, 2):
                                pe.wait_ge(out_ready, val(f - 1))
                            for h in range(HALF):
                                in_product(h, w).then_inc(front_pe, 1)
                        if n == 7:
                            for h in range(HALF):
                                pe.wait_ge(front_act, val(act_at(f, f"xc{h}")))
                                in_product(HALF + h, w).then_inc(front_pe, 1)
                        if n == 10:
                            pe.wait_ge(front_pool, val(pool_at(f, "u")))
                            pe.wait_ge(front_act, val(act_at(f, "z1")))
                            for h in range(HALF):
                                ins = nc.tensor.matmul(misc[0][:, 0:w], w_xp_s[:, h, :], u[par][:, h, 0:w],
                                                       start=(h == 0), stop=(h == HALF - 1))
                            ins.then_inc(front_pe, 1)
                        if n == 11:
                            pe.wait_ge(front_dve, val(dve_at(f, "dt_pair")))
                            for h in range(HALF):
                                if h == 1:
                                    pe.wait_ge(front_dve, val(dve_at(f, "bc_rest")))
                                nc.tensor.matmul(misc[1 - h][:, 0:w], w_dt_pair[:, h * P:(h + 1) * P],
                                                 dt_pair[:, 0:w], start=True, stop=True).then_inc(front_pe, 1)
                    if a is not None:
                        products(1, a, 1 - par, n)
                    if f is None and s is None and t is None and n == 2:
                        turn_rows(NC - 1, (NC - 1) % 2)

            pe.wait_ge(weights_lo, 2)
            rounds(pe.Fori, one_round)


_INS = ["adj_main", "adj_last", "adj_rest", "x", "featT", "w_itemT", "b_item", "w_userT", "b_user", "gcn_w", "gcn_b",
        "ln_g", "ln_b", "w_in", "conv_w", "conv_b", "w_xp", "w_dt4", "dt_rule", "b_dt", "A_log", "D_skip", "w_out"]


def laid_out(inputs):
    import numpy as np
    got = {k.split("_gnn_")[-1] if k[0] == "L" else k: np.asarray(v) for k, v in inputs.items()}
    adjT = got["adj"].T
    top = FULL * P
    whole = (NC - 1) * CW
    return {
        "adj_main": np.ascontiguousarray(
            adjT[:top, :whole].reshape(NG, GT, P, NC - 1, CW).transpose(3, 0, 2, 1, 4)).reshape(NC - 1, NG, P, GT * CW),
        "adj_last": np.ascontiguousarray(
            adjT[:top, whole:].reshape(NG, GT, P, LASTW).transpose(0, 2, 1, 3)).reshape(NG, P, GT * LASTW),
        "adj_rest": np.ascontiguousarray(adjT[top:]),
        "x": got["x"],
        "featT": np.ascontiguousarray(got["item_feat"].T),
        "w_itemT": np.ascontiguousarray(got["W_item"].T),
        "w_userT": np.ascontiguousarray(got["W_user"].T),
        "w_dt4": np.concatenate([got["w_dt"]] * 4),
        "dt_rule": np.repeat(np.array([[0, 1, 0, 1], [1, -1, 0, 1], [0, 1, 1, -1], [1, -1, 1, -1]], np.float32),
                             RANK, axis=0),
        **{k: np.ascontiguousarray(got[k].reshape(HALF, P).T) for k in ("conv_b", "b_dt", "D_skip")},
        **{k: np.ascontiguousarray(got[k]) for k in ("b_item", "b_user", "gcn_w", "gcn_b", "ln_g", "ln_b", "w_in",
                                                     "conv_w", "w_xp", "A_log", "w_out")},
    }


def kernel(**inputs):
    import concourse.bacc as bacc
    from concourse.bass_utils import run_bass_kernel_spmd

    nc = bacc.Bacc("TRN2", target_bir_lowering=False, num_devices=1)
    arrays = laid_out(inputs)
    args = [nc.dram_tensor(f"in_{k}", arrays[k].shape, F32, kind="ExternalInput").ap() for k in _INS]
    out = nc.dram_tensor("out_rows", (NODES, D), F32, kind="ExternalOutput").ap()
    gnn_mamba(nc, *args, out)
    r = run_bass_kernel_spmd(nc, [{f"in_{k}": arrays[k] for k in _INS}], core_ids=[0])
    return r.results[0]["out_rows"]
```
